# Optimizing a Trainium2 kernel written in Bass

```python
import numpy as np
import jax
import jax.numpy as jnp

def _softmax(x, axis=-1):
    return jax.nn.softmax(x, axis=axis)

def _gelu(x):
    return jax.nn.gelu(x, approximate=True)

def _silu(x):
    return jax.nn.silu(x)

def _sigmoid(x):
    return jax.nn.sigmoid(x)

def _layernorm(x, axis=-1, eps=1e-05):
    m = jnp.mean(x, axis=axis, keepdims=True)
    v = jnp.var(x, axis=axis, keepdims=True)
    return (x - m) / jnp.sqrt(v + eps)

def _scatter_add(tgt, idx, src, axis=0):
    return tgt.at[idx].add(src)

def _segment_sum(src, seg, n):
    return jax.ops.segment_sum(src, seg, n)
kernel_name = 'mk_xattn_ffn_d1_seqx_r8_f8f17d'

def setup_inputs(seed: int=0):
    np.random.seed(seed)
    _w = jnp.asarray

    def _rec_inputs():
        import jax
        import jax.numpy as jnp
        _rk = jax.random.key(seed)
        x = -0.0002928 + 1 * jax.random.normal(jax.random.fold_in(_rk, 1), (2, 256, 256), jnp.float32)
        _lenS = 256 - jax.random.randint(jax.random.fold_in(_rk, 7), (2,), 0, max(1, 256 // 4) + 1, jnp.int32)
        _lenS2 = 512 - jax.random.randint(jax.random.fold_in(_rk, 8), (2,), 0, max(1, 512 // 4) + 1, jnp.int32)
        _ctx_512P = jax.random.normal(jax.random.fold_in(_rk, 11), (2, 16, 64), jnp.float32)
        _ctx_512c = jax.random.dirichlet(jax.random.fold_in(_rk, 511), 0.3 * jnp.ones((16,), jnp.float32), (2, 512))
        _ctx_512t = jnp.einsum('bsk,bkd->bsd', _ctx_512c, _ctx_512P)
        _ctx_512t = _ctx_512t * jax.lax.rsqrt(jnp.mean(jnp.square(_ctx_512t)) + 1e-12) * 0.953939
        ctx_512 = 0.000227908 + 0.99994 * (_ctx_512t + 0.3 * jax.random.normal(jax.random.fold_in(_rk, 611), (2, 512, 64), jnp.float32))
        return (x, ctx_512)
    x, ctx_512 = _rec_inputs()

    def _L0_xattn_setup():
        import jax, jax.numpy as jnp
        import numpy as np
        B, S, L = (2, 128, 128)
        DIM_Q, H, K, D_C, D_CQ, R = (256, 16, 128, 64, 192, 64)

        def _rope_tables(length, dim):
            inv = 1.0 / 10000.0 ** (jnp.arange(0, dim, 2, dtype=jnp.float32) / dim)
            f = jnp.arange(length, dtype=jnp.float32)[:, None] * inv[None, :]
            sin = jnp.repeat(jnp.sin(f), 2, axis=-1)
            cos = jnp.repeat(jnp.cos(f), 2, axis=-1)
            return (sin, cos)

        def _rotate_half(x):
            half = x.shape[-1] // 2
            return jnp.concatenate([-x[..., half:], x[..., :half]], axis=-1)

        def _apply_rope(x, sin, cos):
            return x * cos + _rotate_half(x) * sin
        key = jax.random.key(seed)
        ks = jax.random.split(key, 8)
        return {'hidden_q': jax.random.normal(ks[0], (B, S, DIM_Q), jnp.float32), 'kv_c': jax.random.normal(ks[1], (B, L, D_C), jnp.float32), 'Wq': jax.random.normal(ks[2], (H * K, DIM_Q), jnp.float32) / np.sqrt(DIM_Q).astype(np.float32), 'w_kc_q': jax.random.normal(ks[3], (H, K, D_CQ), jnp.float32) / np.sqrt(K).astype(np.float32), 'w_kc_kv': jax.random.normal(ks[4], (H, K, D_C), jnp.float32) / np.sqrt(K).astype(np.float32), 'W_qr': jax.random.normal(ks[5], (H, D_CQ, R), jnp.float32) / np.float32(np.sqrt(D_CQ) * np.sqrt(R)), 'W_kr': jax.random.normal(ks[6], (H, D_C, R), jnp.float32) / np.sqrt(D_C).astype(np.float32), 'Wo': jax.random.normal(ks[7], (DIM_Q, H * K), jnp.float32) / np.sqrt(H * K).astype(np.float32)}
    _L0_xattn_all = _L0_xattn_setup()
    _L0_xattn_in = {k: v for k, v in _L0_xattn_all.items() if k in ('Wq', 'w_kc_q', 'w_kc_kv', 'W_qr', 'W_kr', 'Wo')}
    del _L0_xattn_all

    def _L0_ffn_setup():
        import jax, jax.numpy as jnp
        from jax import lax
        import numpy as np
        B, S, H = (1, 256, 256)
        E = 32
        G = 4
        TOPK_GROUP = 2
        TOP_K = 4
        SCALE = 2.5
        MOE_I = 128

        def _noaux_tc_gate(x_flat, gate_weight, bias):
            T = x_flat.shape[0]
            logits = x_flat.astype(jnp.float32) @ gate_weight.T
            scores = jax.nn.sigmoid(logits)
            scores_for_choice = scores + bias
            grp = scores_for_choice.reshape(T, G, E // G)
            group_scores = lax.top_k(grp, 2)[0].sum(-1)
            gidx = lax.top_k(group_scores, TOPK_GROUP)[1]
            gmask = jax.nn.one_hot(gidx, G, dtype=scores.dtype).sum(1)
            smask = jnp.repeat(gmask, E // G, axis=1)
            masked = jnp.where(smask > 0, scores_for_choice, 0.0)
            topk_idx = lax.top_k(masked, TOP_K)[1]
            tw = jnp.take_along_axis(scores, topk_idx, axis=1)
            tw = tw / (tw.sum(-1, keepdims=True) + 1e-20) * SCALE
            return (topk_idx, tw)

        def _swiglu(x, w_gate, w_up, w_down):
            return jax.nn.silu(x @ w_gate.T) * (x @ w_up.T) @ w_down.T
        key = jax.random.key(seed)
        ks = jax.random.split(key, 9)
        w_scale = 0.02
        return {'hidden_states': jax.random.normal(ks[0], (B, S, H), jnp.float32), 'gate_weight': jax.random.normal(ks[1], (E, H), jnp.float32) * w_scale, 'e_score_correction_bias': jnp.zeros((E,), jnp.float32), 'w1': jax.random.normal(ks[2], (E, MOE_I, H), jnp.float32) * w_scale, 'w3': jax.random.normal(ks[3], (E, MOE_I, H), jnp.float32) * w_scale, 'w2': jax.random.normal(ks[4], (E, H, MOE_I), jnp.float32) * w_scale, 'ws1': jax.random.normal(ks[5], (MOE_I, H), jnp.float32) * w_scale, 'ws3': jax.random.normal(ks[6], (MOE_I, H), jnp.float32) * w_scale, 'ws2': jax.random.normal(ks[7], (H, MOE_I), jnp.float32) * w_scale}
    _L0_ffn_all = _L0_ffn_setup()
    _L0_ffn_in = {k: v for k, v in _L0_ffn_all.items() if k in ('gate_weight', 'e_score_correction_bias', 'w1', 'w3', 'w2', 'ws1', 'ws3', 'ws2')}
    del _L0_ffn_all
    return {'x': x, 'ctx_512': ctx_512, 'L0_xattn_Wq': _L0_xattn_in['Wq'], 'L0_xattn_w_kc_q': _L0_xattn_in['w_kc_q'], 'L0_xattn_w_kc_kv': _L0_xattn_in['w_kc_kv'], 'L0_xattn_W_qr': _L0_xattn_in['W_qr'], 'L0_xattn_W_kr': _L0_xattn_in['W_kr'], 'L0_xattn_Wo': _L0_xattn_in['Wo'], 'L0_ffn_gate_weight': _L0_ffn_in['gate_weight'], 'L0_ffn_e_score_correction_bias': _L0_ffn_in['e_score_correction_bias'], 'L0_ffn_w1': _L0_ffn_in['w1'], 'L0_ffn_w3': _L0_ffn_in['w3'], 'L0_ffn_w2': _L0_ffn_in['w2'], 'L0_ffn_ws1': _L0_ffn_in['ws1'], 'L0_ffn_ws3': _L0_ffn_in['ws3'], 'L0_ffn_ws2': _L0_ffn_in['ws2']}

def reference(x, ctx_512, L0_xattn_Wq, L0_xattn_w_kc_q, L0_xattn_w_kc_kv, L0_xattn_W_qr, L0_xattn_W_kr, L0_xattn_Wo, L0_ffn_gate_weight, L0_ffn_e_score_correction_bias, L0_ffn_w1, L0_ffn_w3, L0_ffn_w2, L0_ffn_ws1, L0_ffn_ws3, L0_ffn_ws2):
    import jax
    import jax.numpy as jnp

    def _L0_xattn_ref(hidden_q, kv_c, Wq, w_kc_q, w_kc_kv, W_qr, W_kr, Wo):
        import jax, jax.numpy as jnp
        import numpy as np
        B, S, L = (2, 128, 128)
        DIM_Q, H, K, D_C, D_CQ, R = (256, 16, 128, 64, 192, 64)

        def _rope_tables(length, dim):
            inv = 1.0 / 10000.0 ** (jnp.arange(0, dim, 2, dtype=jnp.float32) / dim)
            f = jnp.arange(length, dtype=jnp.float32)[:, None] * inv[None, :]
            sin = jnp.repeat(jnp.sin(f), 2, axis=-1)
            cos = jnp.repeat(jnp.cos(f), 2, axis=-1)
            return (sin, cos)

        def _rotate_half(x):
            half = x.shape[-1] // 2
            return jnp.concatenate([-x[..., half:], x[..., :half]], axis=-1)

        def _apply_rope(x, sin, cos):
            return x * cos + _rotate_half(x) * sin
        Bv, Sv, _ = hidden_q.shape
        _, Lv, _ = kv_c.shape
        q_hk = (hidden_q @ Wq.T).reshape(Bv, Sv, H, K)
        q_big = jnp.einsum('bshk,hkq->bshq', q_hk, w_kc_q)
        sin_q, cos_q = _rope_tables(Sv, D_CQ)
        q_big = _apply_rope(q_big, sin_q[None, :, None, :], cos_q[None, :, None, :])
        sin_k, cos_k = _rope_tables(Lv, D_C)
        kv_r = _apply_rope(kv_c, sin_k[None], cos_k[None])
        q_r = jnp.einsum('bshq,hqr->bhsr', q_big, W_qr)
        k_r = jnp.einsum('bld,hdr->bhlr', kv_r, W_kr)
        scores = jnp.einsum('bhsr,bhlr->bhsl', q_r, k_r)
        attn = jax.nn.softmax(scores, axis=-1)
        ctx_c = jnp.einsum('bhsl,bld->bhsd', attn, kv_r)
        ctx_lat = jnp.einsum('bhsd,hkd->bhsk', ctx_c, w_kc_kv)
        ctx = ctx_lat.transpose(0, 2, 1, 3).reshape(Bv, Sv, H * K)
        return ctx @ Wo.T

    def _L0_ffn_ref(hidden_states, gate_weight, e_score_correction_bias, w1, w3, w2, ws1, ws3, ws2):
        import jax, jax.numpy as jnp
        from jax import lax
        import numpy as np
        B, S, H = (1, 256, 256)
        E = 32
        G = 4
        TOPK_GROUP = 2
        TOP_K = 4
        SCALE = 2.5
        MOE_I = 128

        def _noaux_tc_gate(x_flat, gate_weight, bias):
            T = x_flat.shape[0]
            logits = x_flat.astype(jnp.float32) @ gate_weight.T
            scores = jax.nn.sigmoid(logits)
            scores_for_choice = scores + bias
            grp = scores_for_choice.reshape(T, G, E // G)
            group_scores = lax.top_k(grp, 2)[0].sum(-1)
            gidx = lax.top_k(group_scores, TOPK_GROUP)[1]
            gmask = jax.nn.one_hot(gidx, G, dtype=scores.dtype).sum(1)
            smask = jnp.repeat(gmask, E // G, axis=1)
            masked = jnp.where(smask > 0, scores_for_choice, 0.0)
            topk_idx = lax.top_k(masked, TOP_K)[1]
            tw = jnp.take_along_axis(scores, topk_idx, axis=1)
            tw = tw / (tw.sum(-1, keepdims=True) + 1e-20) * SCALE
            return (topk_idx, tw)

        def _swiglu(x, w_gate, w_up, w_down):
            return jax.nn.silu(x @ w_gate.T) * (x @ w_up.T) @ w_down.T
        b, s, h = hidden_states.shape
        x = hidden_states.reshape(-1, h)
        T = x.shape[0]
        topk_idx, topk_w = _noaux_tc_gate(x, gate_weight, e_score_correction_bias)
        combine = jnp.zeros((T, E), x.dtype).at[jnp.arange(T)[:, None], topk_idx].add(topk_w)

        def body(acc, packed):
            w1e, w3e, w2e, ce = packed
            return (acc + ce[:, None] * _swiglu(x, w1e, w3e, w2e), None)
        routed, _ = lax.scan(body, jnp.zeros_like(x), (w1, w3, w2, combine.T))
        shared = _swiglu(x, ws1, ws3, ws2)
        return (routed + shared).reshape(b, s, h)
    x = x + _L0_xattn_ref(_layernorm(x, axis=-1), ctx_512, L0_xattn_Wq, L0_xattn_w_kc_q, L0_xattn_w_kc_kv, L0_xattn_W_qr, L0_xattn_W_kr, L0_xattn_Wo)
    x = x + _L0_ffn_ref(_layernorm(x, axis=-1), L0_ffn_gate_weight, L0_ffn_e_score_correction_bias, L0_ffn_w1, L0_ffn_w3, L0_ffn_w2, L0_ffn_ws1, L0_ffn_ws3, L0_ffn_ws2)
    return x

_drawn_inputs = setup_inputs


def setup_inputs(seed=0):
    import zlib

    import numpy as np

    out = dict(_drawn_inputs(seed))
    spreads = {'L0_ffn_e_score_correction_bias': (0.0, 0.539)}
    factors = {'L0_ffn_gate_weight': 4.904,
     'L0_ffn_w1': 3.979,
     'L0_ffn_w3': 3.903,
     'L0_ffn_w2': 3.916,
     'L0_ffn_ws1': 5.034,
     'L0_ffn_ws3': 4.941,
     'L0_ffn_ws2': 4.962}
    for name, (base, spread) in spreads.items():
        noise = np.random.default_rng([zlib.crc32(name.encode()), seed]).standard_normal(out[name].shape)
        drawn = base * np.exp(spread * noise) if base else spread * noise
        out[name] = jnp.asarray(drawn.astype(out[name].dtype))
    for name, factor in factors.items():
        out[name] = (out[name] * factor).astype(out[name].dtype)
    return out
```

```python
from contextlib import ExitStack

import numpy as np
import concourse.bass as bass
from concourse import mybir

ALU = mybir.AluOpType
ACT = mybir.ActivationFunctionType
AX = mybir.AxisListType
F32 = mybir.dt.float32
F32R = mybir.dt.float32r
U32 = mybir.dt.uint32

P = 128
B, S, D = 2, 256, 256
L, DC = 512, 64
H, K, R, CQ = 16, 128, 64, 192
T = B * S
TT = T // P
ND = D // P
LC = L // P
HALF = CQ // 2
E, G, GE, TOPG, TOPK, I = 32, 4, 8, 2, 4, 128
SCALE = 2.5
EPS = 1e-5

HG = 4
NG = H // HG
NCH = HG * HALF // P
NPG = HG // 2
NP = H // 2
COMBOS = ((0, 0), (1, 0), (1, 1), (2, 1))
NCO = len(COMBOS)
WM = HG * (D + CQ)
WG = NCO * 2 * P + NPG * P
WN = HG * (DC + D)
WGRP = WM + WG + WN
USES = HG + 2 + NPG + 2 * NCH
TILES = H * B * (S // P)
TPG = TILES // NG
WE = 2 * ND * I + D
NX = E + 1
RAW = 2 * WGRP // WE
SPL = 3
CBR = 6


def build(nc, x, ctx_kv, w_attn, w_gate, gate_bias, w_exp, rope_q, rope_kv, ident_in, iota_in, c_dram, out):
    with ExitStack() as stack:
        def sb(name, shape, dt=F32):
            return stack.enter_context(nc.sbuf_tensor(name, shape, dt))

        def sem(name):
            return stack.enter_context(nc.semaphore(name))

        x_sb = sb("x_sb", [P, TT, D])
        xn = sb("xn", [P, TT, D])
        xnT = sb("xnT", [P, 2, ND, T], F32R)
        wring = sb("wring", [P, 2 * WGRP])
        msplit = sb("msplit", [P, SPL * 2 * WE], F32R)
        gmat = sb("gmat", [P, 2, NCO, P])
        nmat = sb("nmat", [P, NP, D])
        rope = sb("rope", [P, NCH, 4, S])
        abuf = sb("abuf", [P, 2, 2, T])
        rtmp = sb("rtmp", [P, 6, T])
        roped = sb("roped", [P, NCH, 2, T])
        qsp = sb("qsp", [P, 4, 2, T], F32R)
        kdup = sb("kdup", [P, 2, B * L], F32R)
        kvs = sb("kvs", [P, B * LC, P], F32R)
        prob = sb("prob", [P, 3, L])
        pT = sb("pT", [P, 2, 2, LC, S], F32R)
        ctmp = sb("ctmp", [P, 2, S])
        ctT = sb("ctT", [P, NP, T])
        kv = sb("kv", [P, B * LC, DC])
        kvr = sb("kvr", [P, B * LC, 2, DC])
        kvtab = sb("kvtab", [P, LC, 2, DC])
        ident = sb("ident", [P, P])
        iota = sb("iota", [P, E])
        gateT = sb("gateT", [P, ND, E])
        bias = sb("bias", [P, E])
        stat = sb("stat", [P, 2 * TT, 6])
        mv = sb("mv", [P, 2 * TT, 2])
        std = sb("std", [P, 2 * TT, 1])
        rstd = sb("rstd", [P, 2 * TT, 1])
        nmax = sb("nmax", [P, TILES])
        psum_e = sb("psum_e", [P, TILES])
        rsum = sb("rsum", [P, TILES])
        sc = sb("sc", [P, TT, E])
        sfc = sb("sfc", [P, TT, E])
        g8 = sb("g8", [P, TT, G, 8])
        gs = sb("gs", [P, TT, 8])
        gtop = sb("gtop", [P, TT, 8])
        gidx = sb("gidx", [P, TT, 8], U32)
        gidxf = sb("gidxf", [P, TT, 8])
        gmask = sb("gmask", [P, TT, G])
        masked = sb("masked", [P, TT, E])
        etop = sb("etop", [P, TT, 8])
        eidx = sb("eidx", [P, TT, 8], U32)
        eidxf = sb("eidxf", [P, TT, 8])
        emask = sb("emask", [P, TT, E])
        esel = sb("esel", [P, TT, E])
        wsum = sb("wsum", [P, TT, 3])
        comb = sb("comb", [P, TT, E])
        combT = prob[0:E, 2, :]
        epsc = sb("epsc", [P, 1])

        bank = [stack.enter_context(nc.psum_tensor(f"bank{i}", [P, 512], F32)) for i in range(8)]
        work = bank[0:2]
        qr_ps = bank[2]
        s_ps = bank[3:5]
        t_ps = bank[5:7]
        pv_ps = bank[7]
        h_ps = bank[0:4]
        r_ps = bank[4]
        acc_ps = bank[5:7]
        g_ps = bank[7]

        def half_of(g):
            return (g % 2) * WGRP

        def wq(g, i, dc):
            a = half_of(g) + i * D + dc * P
            return wring[:, a:a + P]

        def wkcq(g, i):
            a = half_of(g) + HG * D + i * CQ
            return wring[:, a:a + CQ]

        def wqrT(g, m, ab):
            a = half_of(g) + WM + (m * 2 + ab) * P
            return wring[:, a:a + P]

        def wkrT(g, j):
            a = half_of(g) + WM + NCO * 2 * P + j * P
            return wring[:, a:a + P]

        def wkv(g, i):
            a = half_of(g) + WM + WG + i * DC
            return wring[:, a:a + DC]

        def woT(g, i):
            a = half_of(g) + WM + WG + HG * DC + i * D
            return wring[:, a:a + D]

        m_v = msplit[:, 0:2 * ND * 2 * HG * HALF].rearrange("p (s d a n) -> p s d a n", s=2, d=ND, a=2)
        w_v = msplit[:, :].rearrange("p (r s n) -> p r s n", r=SPL, s=2)
        raw_v = wring[:, 0:RAW * WE].rearrange("p (r n) -> p r n", r=RAW)
        roped_flat = roped[:, :, :, :].rearrange("p c a t -> p (c a) t")
        pT_flat = pT[:, :, :, :, :].rearrange("p s b c q -> p (s b) (c q)")

        xT_f = abuf[:, :, :, 0:P]
        xn_out = [prob[:, 0, :], prob[:, 1, :]]

        def f(ap):
            return ap.bitcast(F32)

        d_x = sem("d_x"); d_kv = sem("d_kv"); d_const = sem("d_const"); d_rope = sem("d_rope"); d_gate = sem("d_gate")
        d_wm = [sem(f"d_wm{i}") for i in range(2)]
        d_wg = [sem(f"d_wg{i}") for i in range(2)]
        d_wn = [sem(f"d_wn{i}") for i in range(2)]
        d_raw = [sem(f"d_raw{i}") for i in range(RAW)]
        d_ct = sem("d_ct"); d_cb = [sem(f"d_cb{i}") for i in range(CBR)]
        d_out = sem("d_out")
        chain_v = sem("chain_v")
        chain_p = sem("chain_p")
        ln_std = sem("ln_std"); ln_mv = sem("ln_mv"); ln_xn = sem("ln_xn")
        kv_roped = sem("kv_roped"); kv_split = sem("kv_split")
        xT_mm = sem("xT_mm"); xT_hi = sem("xT_hi"); xT_lo = sem("xT_lo")
        kT_mm = sem("kT_mm"); kT_hi = sem("kT_hi"); kT_lo = sem("kT_lo")
        wk_full = sem("wk_full"); wk_out = sem("wk_out"); m_lo = sem("m_lo")
        rope_a = sem("rope_a"); rope_p = sem("rope_p")
        qr_mm = sem("qr_mm"); q_hi = sem("q_hi"); q_lo = sem("q_lo")
        s_mm = sem("s_mm"); s_max = sem("s_max"); s_exp = sem("s_exp"); s_inv = sem("s_inv"); s_norm = sem("s_norm")
        t_mm = sem("t_mm"); t_hi = sem("t_hi"); t_lo = sem("t_lo")
        pv_mm = sem("pv_mm"); c_half = sem("c_half"); c_sum = sem("c_sum")
        o_mm = sem("o_mm"); x1_done = sem("x1_done"); x2_std = sem("x2_std"); x2_mv = sem("x2_mv"); x2_n = sem("x2_n")
        y_mm = sem("y_mm"); y_f = sem("y_f"); y_hi = sem("y_hi"); y_lo = sem("y_lo")
        lg_mm = sem("lg_mm"); lg_sc = sem("lg_sc"); cmb = sem("cmb"); ct_mm = sem("ct_mm"); ct_sb = sem("ct_sb")
        wx_hi = sem("wx_hi"); wx_lo = sem("wx_lo")
        h1_mm = sem("h1_mm"); h3_mm = sem("h3_mm"); silu = sem("silu"); sw = sem("sw"); gated = sem("gated")
        g_hi = sem("g_hi"); g_lo = sem("g_lo"); w2_mm = sem("w2_mm"); fin = [sem(f"fin{i}") for i in range(ND)]

        PLAN = {0: ["M0", "M1"], 1: ["M2", "M3"], 2: ["G0", "G1"], 3: ["N0", "N1"], 4: ["Q0"], 6: ["Q1"], 8: ["Q2"],
                11: ["R0"], 15: ["R1"]}

        def steps(t):
            g = t // TPG + 1
            return [(g, s[0], int(s[1])) for s in PLAN.get(t % TPG, [])] if g < NG else []

        PROLOGUE = [(0, s[0], int(s[1])) for s in ("Q0", "Q1", "Q2", "R0", "R1")]

        block = stack.enter_context(nc.Block())

        def rope_half(eng, alu, link, n, c, ab):
            own, other = abuf[:, n % 2, ab, :], abuf[:, n % 2, 1 - ab, :]
            cos = rope[:, c, 2 * ab, :].unsqueeze(1).to_broadcast([P, B, S])
            sin = rope[:, c, 2 * ab + 1, :].unsqueeze(1).to_broadcast([P, B, S])
            t0, t1 = rtmp[:, 2 * ab, :], rtmp[:, 2 * ab + 1, :]
            eng.tensor_tensor(t0.rearrange("p (b s) -> p b s", b=B), own.rearrange("p (b s) -> p b s", b=B), cos, alu.mult)
            link(eng.tensor_tensor(t1.rearrange("p (b s) -> p b s", b=B), other.rearrange("p (b s) -> p b s", b=B), sin,
                                   alu.mult))
            return eng.tensor_tensor(roped[:, c, ab, :], t0, t1, alu.add)

        @block.sync
        def _(sp):
            sp.dma_start(x_sb[:, :, :], x).then_inc(d_x, 16)
            sp.dma_start(ident[:, :], ident_in).then_inc(d_const, 16)

            def load_group(g, part):
                a, n, s = {"m": (0, WM, d_wm), "g": (WM, WG, d_wg), "n": (WM + WG, WN, d_wn)}[part]
                sp.dma_start(wring[:, half_of(g) + a:half_of(g) + a + n], w_attn[g, :, a:a + n]).then_inc(s[g % 2], 16)

            load_group(0, "m")
            sp.dma_start(kv[:, :, :], ctx_kv).then_inc(d_kv, 16)
            sp.dma_start(kvtab[:, :, :, :], rope_kv).then_inc(d_kv, 16)
            sp.dma_start(rope[:, :, :, :], rope_q).then_inc(d_rope, 16)
            load_group(0, "g")
            load_group(0, "n")
            for part in "mgn":
                load_group(1, part)
            sp.dma_start(gateT[:, :, :], w_gate).then_inc(d_gate, 16)
            sp.dma_start(bias[:, :], gate_bias).then_inc(d_gate, 16)
            sp.dma_start(iota[:, :], iota_in).then_inc(d_gate, 16)
            for g in range(2, NG):
                sp.wait_ge(wk_full, USES * (g - 2) + HG + 2 + NPG)
                for part in "mgn":
                    load_group(g, part)
            for n in range(NX):
                if n < RAW:
                    last = NG - 2 if (n + 1) * WE <= WGRP else NG - 1
                    sp.wait_ge(wk_full, USES * last + HG + 2 + NPG)
                else:
                    sp.wait_ge(wx_lo, n - RAW + 1)
                sp.dma_start(raw_v[:, n % RAW, :], w_exp[n]).then_inc(d_raw[n % RAW], 16)
                if n == RAW - 1:
                    sp.wait_ge(ct_sb, TT)
                    sp.dma_start(c_dram, combT).then_inc(d_ct, 16)
                    sp.wait_ge(d_ct, 16)
                    for e in range(CBR):
                        sp.dma_start(roped_flat[:, e, :], c_dram[e:e + 1, :].to_broadcast([P, T])).then_inc(d_cb[e], 16)
                if n >= RAW:
                    e = n - RAW + CBR
                    if e < E:
                        sp.wait_ge(sw, e - CBR + 1)
                        sp.dma_start(roped_flat[:, e % CBR, :], c_dram[e:e + 1, :].to_broadcast([P, T])) \
                          .then_inc(d_cb[e % CBR], 16)
            for e in range(NX - RAW + CBR, E):
                sp.wait_ge(sw, e - CBR + 1)
                sp.dma_start(roped_flat[:, e % CBR, :], c_dram[e:e + 1, :].to_broadcast([P, T])) \
                  .then_inc(d_cb[e % CBR], 16)
            for dc in range(ND):
                sp.wait_ge(fin[dc], 1)
                sp.dma_start(out[dc * P:(dc + 1) * P, :], xn_out[dc]).then_inc(d_out, 16)
            sp.wait_ge(d_out, 16 * ND)

        @block.tensor
        def _(pe):
            def split3(out_ap, a_hi, a_lo, b_hi, b_lo, first, last):
                pe.matmul(out_ap, a_hi, b_hi, start=first, stop=False)
                pe.matmul(out_ap, a_hi, b_lo, start=False, stop=False)
                return pe.matmul(out_ap, a_lo, b_hi, start=False, stop=last)

            def bank_free(u):
                if u < 2:
                    return
                g, k = divmod(u - 2, USES)
                if k < HG:
                    pe.wait_ge(m_lo, HG * g + k + 1)
                else:
                    pe.wait_ge(wk_out, u - 1)

            def step(g, kind, i):
                if kind == "M":
                    u = USES * g + i
                    bank_free(u)
                    pe.wait_ge(d_wm[g % 2], 16 * (g // 2 + 1))
                    for dc in range(ND):
                        mm = pe.matmul(work[u % 2][:, dc * CQ:(dc + 1) * CQ], wq(g, i, dc), wkcq(g, i),
                                       start=True, stop=True)
                    mm.then_inc(wk_full, 1)
                elif kind == "G":
                    u = USES * g + HG + i
                    bank_free(u)
                    pe.wait_ge(d_wg[g % 2], 16 * (g // 2 + 1))
                    for m, (_, j) in enumerate(COMBOS):
                        mm = pe.matmul(work[u % 2][:, m * P:(m + 1) * P], wqrT(g, m, i), wkrT(g, j),
                                       start=True, stop=True)
                    mm.then_inc(wk_full, 1)
                elif kind == "N":
                    u = USES * g + HG + 2 + i
                    bank_free(u)
                    pe.wait_ge(d_wn[g % 2], 16 * (g // 2 + 1))
                    for k in range(2):
                        mm = pe.matmul(work[u % 2][k * DC:(k + 1) * DC, 0:D], wkv(g, 2 * i + k), woT(g, 2 * i + k),
                                       start=True, stop=True)
                    mm.then_inc(wk_full, 1)
                elif kind == "Q":
                    for ab in range(2):
                        u = USES * g + HG + 2 + NPG + 2 * i + ab
                        bank_free(u)
                        if i == 0 and ab == 0:
                            pe.wait_ge(m_lo, HG * (g + 1))
                            pe.wait_ge(xT_lo, ND)
                        for dc in range(ND):
                            cols = slice(i * P, (i + 1) * P)
                            mm = split3(work[u % 2][:, :], m_v[:, 0, dc, ab, cols], m_v[:, 1, dc, ab, cols],
                                        xnT[:, 0, dc, :], xnT[:, 1, dc, :], dc == 0, dc == ND - 1)
                        mm.then_inc(wk_full, 1)
                else:
                    p = NPG * g + i
                    if p >= 1:
                        pe.wait_ge(q_lo, p)
                    pe.wait_ge(wk_out, USES * g + HG + 2)
                    pe.wait_ge(rope_p, NCH * g + i + 2)
                    if g == 0:
                        pe.wait_ge(rope_a, i + 2)
                    todo = [(m, c, ab) for m, (c, j) in enumerate(COMBOS) if j == i for ab in range(2)]
                    for n, (m, c, ab) in enumerate(todo):
                        mm = pe.matmul(qr_ps[:, :], gmat[:, ab, m, :], roped[:, c, ab, :],
                                       start=(n == 0), stop=(n == len(todo) - 1))
                    mm.then_inc(qr_mm, 1)

            def scores(t):
                h, b, st = t // 4, (t // 2) % 2, t % 2
                pe.wait_ge(q_lo, h // 2 + 1)
                if t == 0:
                    pe.wait_ge(kT_lo, 2)
                if t >= 2:
                    pe.wait_ge(s_exp, t - 1)
                q = qsp[:, (h // 2) % 4, h % 2, b * S + st * P:b * S + (st + 1) * P]
                pe.matmul(s_ps[t % 2][:, :], q, kdup[:, 0, b * L:(b + 1) * L], start=True, stop=False)
                pe.matmul(s_ps[t % 2][:, :], q, kdup[:, 1, b * L:(b + 1) * L], start=False, stop=True) \
                  .then_inc(s_mm, 1)

            def transposes(t):
                pe.wait_ge(s_norm, t + 1)
                if t >= 2:
                    pe.wait_ge(t_lo, t - 1)
                for lc in range(LC):
                    mm = pe.transpose(t_ps[t % 2][:, lc * P:(lc + 1) * P], prob[:, t % 3, lc * P:(lc + 1) * P],
                                      ident[:, :])
                mm.then_inc(t_mm, 1)

            def attend(hb):
                b = hb % 2
                pe.wait_ge(t_lo, 2 * hb + 2)
                if hb == 0:
                    pe.wait_ge(kv_split, 2)
                if hb >= 1:
                    pe.wait_ge(c_sum, hb)
                for n in range(2 * LC):
                    lc, hl = n // 2, n % 2
                    mm = pe.matmul(pv_ps[:, b * S:(b + 1) * S], kvs[:, b * LC + lc, :], pT[:, hl, hb % 2, lc, :],
                                   start=(n == 0), stop=(n == 2 * LC - 1))
                mm.then_inc(pv_mm, 1)

            pe.wait_ge(d_const, 16)
            for i in range(HG):
                step(0, "M", i)
            for tt in range(TT):
                pe.wait_ge(ln_xn, tt + 1)
                for dc in range(ND):
                    mm = pe.transpose(t_ps[dc][:, tt * P:(tt + 1) * P], xn[:, tt, dc * P:(dc + 1) * P], ident[:, :])
            mm.then_inc(xT_mm, 1)
            for i in range(2):
                step(0, "G", i)
            for i in range(NPG):
                step(0, "N", i)
            step(*PROLOGUE[0])
            pe.wait_ge(kv_roped, 1)
            for n in range(B * LC):
                mm = pe.transpose(s_ps[n // LC][:, (n % LC) * P:(n % LC + 1) * P],
                                  kvr[:, n, :, :].rearrange("p a c -> p (a c)"), ident[:, :])
            mm.then_inc(kT_mm, 1)
            for s in PROLOGUE[1:]:
                step(*s)
            pe.wait_ge(kT_lo, 2)
            scores(0)
            scores(1)
            for t in range(TILES):
                if t + 2 < TILES:
                    scores(t + 2)
                for s in steps(t):
                    step(*s)
                transposes(t)
                if t % 2 == 0 and t >= 2:
                    attend(t // 2 - 1)
            attend(TILES // 2 - 1)

            pe.wait_ge(c_sum, TILES // 2)
            pe.wait_ge(wk_out, USES * (NG - 1) + USES)
            for tt in range(TT):
                for p in range(NP):
                    mm = pe.matmul(h_ps[tt][:, 0:D], ctT[:, p, tt * P:(tt + 1) * P], nmat[:, p, :],
                                   start=(p == 0), stop=(p == NP - 1))
                mm.then_inc(o_mm, 1)

            def rows_T(tt):
                pe.wait_ge(x2_n, tt + 1)
                if tt >= 1:
                    pe.wait_ge(y_lo, tt)
                    pe.wait_ge(y_f, tt)
                for dc in range(ND):
                    mm = pe.transpose(r_ps[:, dc * P:(dc + 1) * P], xn[:, tt, dc * P:(dc + 1) * P], ident[:, :])
                mm.then_inc(y_mm, 1)

            def seed(tt):
                for dc in range(ND):
                    pe.matmul(acc_ps[dc][:, tt * P:(tt + 1) * P], x_sb[:, tt, dc * P:(dc + 1) * P], ident[:, :],
                              start=(tt == 0), stop=False, skip_group_check=True)

            def logits(tt):
                pe.wait_ge(y_f, tt + 1)
                if tt == 0:
                    pe.wait_ge(d_gate, 48)
                for dc in range(ND):
                    mm = pe.matmul(g_ps[:, tt * E:(tt + 1) * E], xT_f[:, tt % 2, dc, :], gateT[:, dc, :],
                                   start=(dc == 0), stop=(dc == ND - 1))
                mm.then_inc(lg_mm, 1)

            def expert_in(n):
                if n >= 2:
                    pe.wait_ge(gated, n - 1)
                pe.wait_ge(wx_lo, n + 1)
                pe.wait_ge(wx_hi, n + 1)
                for w, signal in ((0, h1_mm), (1, h3_mm)):
                    for dc in range(ND):
                        a = (w * ND + dc) * I
                        mm = split3(h_ps[2 * (n % 2) + w][:, :], w_v[:, n % SPL, 0, a:a + I], w_v[:, n % SPL, 1, a:a + I],
                                    xnT[:, 0, dc, :], xnT[:, 1, dc, :], dc == 0, dc == ND - 1)
                    mm.then_inc(signal, 1)

            def expert_out(n):
                pe.wait_ge(g_lo, n + 1)
                for dc in range(ND):
                    a = 2 * ND * I + dc * P
                    w_hi, w_lo = w_v[:, n % SPL, 0, a:a + P], w_v[:, n % SPL, 1, a:a + P]
                    gh, gl = pT_flat[:, n % 2, 0:T], pT_flat[:, 2 + n % 2, 0:T]
                    for k, (wp, gp) in enumerate(((w_hi, gh), (w_hi, gl), (w_lo, gh))):
                        mm = pe.matmul(acc_ps[dc][:, :], wp, gp, start=False, stop=(n == NX - 1 and k == 2),
                                       skip_group_check=True)
                mm.then_inc(w2_mm, 1)

            for tt in range(TT):
                rows_T(tt)
                seed(tt)
                logits(tt)
            pe.wait_ge(y_lo, TT)
            pe.wait_ge(y_hi, TT)
            pe.wait_ge(x1_done, TT)
            expert_in(0)
            for tt in range(TT):
                pe.wait_ge(cmb, tt + 1)
                pe.wait_ge(lg_sc, TT)
                if tt >= 1:
                    pe.wait_ge(ct_sb, tt)
                pe.transpose(g_ps[0:E, tt * P:(tt + 1) * P], comb[:, tt, :], ident[:, :]).then_inc(ct_mm, 1)
            for n in range(NX):
                if n + 1 < NX:
                    expert_in(n + 1)
                expert_out(n)

        @block.scalar
        def _(act):
            for tt in range(TT):
                act.wait_ge(ln_mv, tt + 1)
                act.activation(std[:, tt, :], mv[:, tt, 1:2], ACT.Sqrt, bias=epsc[:, :]).then_inc(ln_std, 1)

            def step(g, kind, i):
                if kind == "M":
                    u = USES * g + i
                    act.wait_ge(wk_full, u + 1)
                    if g >= 1:
                        act.wait_ge(wk_full, USES * g)
                    act.copy(m_v[:, 0, :, :, i * HALF:(i + 1) * HALF],
                             work[u % 2][:, 0:ND * CQ].rearrange("p (d a n) -> p d a n", d=ND, a=2)).then_inc(wk_out, 1)
                elif kind == "G":
                    u = USES * g + HG + i
                    act.wait_ge(wk_full, u + 1)
                    if g >= 1:
                        act.wait_ge(qr_mm, NPG * g)
                    act.copy(gmat[:, i, :, :].rearrange("p m n -> p (m n)"), work[u % 2][:, :]).then_inc(wk_out, 1)
                elif kind == "N":
                    u = USES * g + HG + 2 + i
                    act.wait_ge(wk_full, u + 1)
                    act.copy(nmat[:, NPG * g + i, :], work[u % 2][:, 0:D]).then_inc(wk_out, 1)
                elif kind == "Q":
                    n = NCH * g + i
                    for ab in range(2):
                        u = USES * g + HG + 2 + NPG + 2 * i + ab
                        act.wait_ge(wk_full, u + 1)
                        if n >= 2:
                            act.wait_ge(rope_p, n - 1)
                            if n - 2 < NCH:
                                act.wait_ge(rope_a, n - 1)
                        act.copy(abuf[:, n % 2, ab, :], work[u % 2][:, :]).then_inc(wk_out, 1)
                else:
                    p = NPG * g + i
                    act.wait_ge(qr_mm, p + 1)
                    if p >= 4:
                        act.wait_ge(s_mm, 8 * (p - 3))
                    act.copy(qsp[0:R, p % 4, 0, :], qr_ps[0:R, :]).then_inc(q_hi, 1)
                    act.copy(qsp[R:P, p % 4, 1, :], qr_ps[R:P, :]).then_inc(q_hi, 1)

            def exps(t):
                act.wait_ge(s_max, t + 1)
                if t >= 3:
                    act.wait_ge(t_mm, t - 2)
                act.activation(prob[:, t % 3, :], s_ps[t % 2][:, :], ACT.Exp, bias=nmax[:, t:t + 1],
                               accum_out=psum_e[:, t:t + 1]).then_inc(s_exp, 1)

            def prob_hi(t):
                hb = t // 2
                act.wait_ge(t_mm, t + 1)
                if hb >= 2:
                    act.wait_ge(pv_mm, hb - 1)
                act.copy(pT[:, 0, hb % 2, :, (t % 2) * P:(t % 2 + 1) * P],
                         t_ps[t % 2][:, :].rearrange("p (c q) -> p c q", c=LC)).then_inc(t_hi, 1)

            def ctx_half(hb):
                h, b = divmod(hb, 2)
                act.wait_ge(pv_mm, hb + 1)
                if hb >= 2:
                    act.wait_ge(c_sum, hb - 1)
                dst, src = (0, DC) if h % 2 == 0 else (DC, 0)
                act.copy(ctmp[dst:dst + DC, hb % 2, :], pv_ps[src:src + DC, b * S:(b + 1) * S]).then_inc(c_half, 1)

            for i in range(HG):
                step(0, "M", i)
            act.wait_ge(xT_mm, 1)
            for dc in range(ND):
                act.copy(xnT[:, 0, dc, :], t_ps[dc][:, :]).then_inc(xT_hi, 1)
            for i in range(2):
                step(0, "G", i)
            for i in range(NPG):
                step(0, "N", i)
            step(*PROLOGUE[0])
            act.wait_ge(kT_mm, 1)
            for n in range(2):
                act.copy(kdup[:, 0, n * L:(n + 1) * L], s_ps[n][:, :]).then_inc(kT_hi, 1)
            for s in PROLOGUE[1:]:
                step(*s)
            exps(0)
            exps(1)
            for t in range(TILES):
                if t + 2 < TILES:
                    exps(t + 2)
                for s in steps(t):
                    step(*s)
                prob_hi(t)
                if t % 2 == 1 and t >= 3:
                    ctx_half((t - 3) // 2)
            ctx_half(TILES // 2 - 1)

            def row_std(tt):
                act.wait_ge(x2_mv, tt + 1)
                act.activation(std[:, TT + tt, :], mv[:, TT + tt, 1:2], ACT.Sqrt, bias=epsc[:, :]).then_inc(x2_std, 1)

            def row_copy(tt):
                act.wait_ge(y_mm, tt + 1)
                if tt >= 2:
                    act.wait_ge(lg_mm, tt - 1)
                act.copy(xT_f[:, tt % 2, :, :], r_ps[:, 0:ND * P].rearrange("p (d q) -> p d q", d=ND)).then_inc(y_f, 1)

            for tt in range(TT):
                row_std(tt)
            for tt in range(TT):
                row_copy(tt)
            for tt in range(TT):
                act.wait_ge(lg_mm, TT)
                act.activation(sc[:, tt, :], g_ps[:, tt * E:(tt + 1) * E], ACT.Sigmoid).then_inc(lg_sc, 1)

            def silus(n):
                act.wait_ge(h1_mm, n + 1)
                if n >= 2:
                    act.wait_ge(sw, n - 2)
                    act.wait_ge(gated, n - 1)
                act.activation(rtmp[:, n % 2, :], h_ps[2 * (n % 2)][:, :], ACT.Silu).then_inc(silu, 1)

            def gate_hi(n):
                act.wait_ge(gated, n + 1)
                if n >= 2:
                    act.wait_ge(w2_mm, n - 1)
                act.copy(pT_flat[:, n % 2, 0:T], rtmp[:, 4 + n % 2, :]).then_inc(g_hi, 1)

            silus(0)
            gate_hi(0)
            for tt in range(TT):
                act.wait_ge(ct_mm, tt + 1)
                act.copy(combT[:, tt * P:(tt + 1) * P], g_ps[0:E, tt * P:(tt + 1) * P]).then_inc(ct_sb, 1)
            for n in range(1, NX):
                silus(n)
                gate_hi(n)
            act.wait_ge(w2_mm, NX)
            act.copy(prob[:, 0, :], acc_ps[0][:, :]).then_inc(fin[0], 1)

        @block.vector
        def _(dve):
            links = [0]

            def link(ins):
                links[0] += 1
                ins.then_inc(chain_v, 1)
                dve.wait_ge(chain_v, links[0])

            def norm_stats(tt, o, signal):
                link(dve.bn_stats(stat[:, o + tt, :], x_sb[:, tt, :]))
                dve.bn_aggr(mv[:, o + tt, :], stat[:, o + tt, :]).then_inc(signal, 1)

            def norm_rows(tt, o, got, signal):
                dve.wait_ge(got, tt + 1)
                link(dve.reciprocal(rstd[:, o + tt, :], std[:, o + tt, :]))
                dve.tensor_scalar(xn[:, tt, :], x_sb[:, tt, :], mv[:, o + tt, 0:1], rstd[:, o + tt, :],
                                  ALU.subtract, ALU.mult).then_inc(signal, 1)

            dve.memset(gs[:, :, :], -3.0e38)
            link(dve.memset(epsc[:, :], EPS))
            dve.wait_ge(d_x, 16)
            for tt in range(TT):
                norm_stats(tt, 0, ln_mv)
            for tt in range(TT):
                norm_rows(tt, 0, ln_std, ln_xn)

            def step(g, kind, i):
                if kind == "M":
                    u = USES * g + i
                    dve.wait_ge(wk_out, u + 1)
                    dve.tensor_tensor(m_v[:, 1, :, :, i * HALF:(i + 1) * HALF],
                                      work[u % 2][:, 0:ND * CQ].rearrange("p (d a n) -> p d a n", d=ND, a=2),
                                      f(m_v[:, 0, :, :, i * HALF:(i + 1) * HALF]), ALU.subtract).then_inc(m_lo, 1)
                elif kind == "Q" and g == 0:
                    n = i
                    dve.wait_ge(d_rope, 16)
                    dve.wait_ge(wk_out, HG + 2 + NPG + 2 * i + 2)
                    rope_half(dve, ALU, link, n, i, 0).then_inc(rope_a, 1)
                    dve.wait_ge(rope_a, n + 1)
                elif kind == "R":
                    p = NPG * g + i
                    dve.wait_ge(q_hi, 2 * p + 2)
                    dve.tensor_tensor(qsp[R:P, p % 4, 0, :], qr_ps[0:R, :], f(qsp[0:R, p % 4, 0, :]), ALU.subtract)
                    dve.tensor_tensor(qsp[0:R, p % 4, 1, :], qr_ps[R:P, :], f(qsp[R:P, p % 4, 1, :]), ALU.subtract) \
                       .then_inc(q_lo, 1)

            def row_max(t):
                dve.wait_ge(s_mm, t + 1)
                dve.tensor_reduce(nmax[:, t:t + 1], s_ps[t % 2][:, :], AX.X, ALU.max, negate=True).then_inc(s_max, 1)

            def normalise(t):
                dve.wait_ge(s_exp, t + 1)
                dve.reciprocal(rsum[:, t:t + 1], psum_e[:, t:t + 1]).then_inc(s_inv, 1)
                dve.wait_ge(s_inv, t + 1)
                dve.tensor_scalar(prob[:, t % 3, :], prob[:, t % 3, :], rsum[:, t:t + 1], None, ALU.mult) \
                   .then_inc(s_norm, 1)

            def prob_lo(t):
                hb, q = t // 2, slice((t % 2) * P, (t % 2 + 1) * P)
                dve.wait_ge(t_hi, t + 1)
                dve.tensor_tensor(pT[:, 1, hb % 2, :, q], t_ps[t % 2][:, :].rearrange("p (c q) -> p c q", c=LC),
                                  f(pT[:, 0, hb % 2, :, q]), ALU.subtract).then_inc(t_lo, 1)

            def ctx_sum(hb):
                h, b = divmod(hb, 2)
                dve.wait_ge(c_half, hb + 1)
                r = (h % 2) * DC
                dve.tensor_tensor(ctT[r:r + DC, h // 2, b * S:(b + 1) * S], pv_ps[r:r + DC, b * S:(b + 1) * S],
                                  ctmp[r:r + DC, hb % 2, :], ALU.add).then_inc(c_sum, 1)

            for i in range(HG):
                step(0, "M", i)
            for dc in range(ND):
                dve.wait_ge(xT_hi, dc + 1)
                dve.tensor_tensor(xnT[:, 1, dc, :], t_ps[dc][:, :], f(xnT[:, 0, dc, :]), ALU.subtract).then_inc(xT_lo, 1)
            dve.wait_ge(kv_roped, 1)
            dve.tensor_copy(kvs[:, :, 0:DC], kvr[:, :, 0, :]).then_inc(kv_split, 1)
            dve.wait_ge(kv_split, 1)
            dve.tensor_tensor(kvs[:, :, DC:P], kvr[:, :, 0, :], f(kvs[:, :, 0:DC]), ALU.subtract).then_inc(kv_split, 1)
            step(*PROLOGUE[0])
            for n in range(2):
                dve.wait_ge(kT_hi, n + 1)
                dve.tensor_tensor(kdup[:, 1, n * L:(n + 1) * L], s_ps[n][:, :], f(kdup[:, 0, n * L:(n + 1) * L]),
                                  ALU.subtract).then_inc(kT_lo, 1)
            for s in PROLOGUE[1:]:
                step(*s)
            row_max(0)
            row_max(1)
            normalise(0)
            for t in range(TILES):
                if t + 2 < TILES:
                    row_max(t + 2)
                if t + 1 < TILES:
                    normalise(t + 1)
                for s in steps(t):
                    step(*s)
                prob_lo(t)
                if t % 2 == 1 and t >= 3:
                    ctx_sum((t - 3) // 2)
            ctx_sum(TILES // 2 - 1)

            def weight_hi(n):
                dve.wait_ge(d_raw[n % RAW], 16 * (n // RAW + 1))
                if n == 0:
                    dve.wait_ge(wk_full, USES * NG)
                if n >= SPL:
                    dve.wait_ge(w2_mm, n - SPL + 1)
                dve.tensor_copy(w_v[:, n % SPL, 0, :], raw_v[:, n % RAW, :]).then_inc(wx_hi, 1)

            weight_hi(0)
            weight_hi(1)
            for tt in range(TT):
                dve.wait_ge(o_mm, tt + 1)
                link(dve.tensor_tensor(x_sb[:, tt, :], h_ps[tt][:, 0:D], x_sb[:, tt, :], ALU.add))
                norm_stats(tt, TT, x2_mv)
            dve.wait_ge(x2_mv, TT)
            for tt in range(TT):
                norm_rows(tt, TT, x2_std, x2_n)
            for tt in range(TT):
                dve.wait_ge(y_f, tt + 1)
                ps = r_ps[:, 0:ND * P].rearrange("p (d q) -> p d q", d=ND)
                hi, lo = xnT[:, 0, :, tt * P:(tt + 1) * P], xnT[:, 1, :, tt * P:(tt + 1) * P]
                dve.tensor_copy(hi, ps).then_inc(y_hi, 1)
                dve.wait_ge(y_hi, tt + 1)
                dve.tensor_tensor(lo, ps, f(hi), ALU.subtract).then_inc(y_lo, 1)
            dve.memset(epsc[:, :], EPS).then_inc(x1_done, TT)

            def route(tt):
                dve.wait_ge(lg_sc, tt + 1)
                link(dve.tensor_tensor(sfc[:, tt, :], sc[:, tt, :], bias[:, :], ALU.add))
                for g in range(G):
                    last = dve.max(g8[:, tt, g, :], sfc[:, tt, g * GE:(g + 1) * GE])
                link(last)
                link(dve.tensor_tensor(gs[:, tt, 0:G], g8[:, tt, :, 0], g8[:, tt, :, 1], ALU.add))
                link(dve.max(gtop[:, tt, :], gs[:, tt, :]))
                link(dve.max_index(gidx[:, tt, :], gtop[:, tt, :], gs[:, tt, :]))
                link(dve.tensor_copy(gidxf[:, tt, :], gidx[:, tt, :]))
                link(dve.tensor_scalar(gmask[:, tt, :], iota[:, 0:G], gidxf[:, tt, 0:1], None, ALU.is_equal))
                for k in range(1, TOPG):
                    link(dve.scalar_tensor_tensor(gmask[:, tt, :], iota[:, 0:G], gidxf[:, tt, k:k + 1], gmask[:, tt, :],
                                                  ALU.is_equal, ALU.add))
                link(dve.tensor_tensor(masked[:, tt, :].rearrange("p (g e) -> p g e", g=G),
                                       sfc[:, tt, :].rearrange("p (g e) -> p g e", g=G),
                                       gmask[:, tt, :].unsqueeze(2).to_broadcast([P, G, GE]), ALU.mult))
                link(dve.max(etop[:, tt, :], masked[:, tt, :]))
                link(dve.max_index(eidx[:, tt, :], etop[:, tt, :], masked[:, tt, :]))
                link(dve.tensor_copy(eidxf[:, tt, :], eidx[:, tt, :]))
                link(dve.tensor_scalar(emask[:, tt, :], iota[:, :], eidxf[:, tt, 0:1], None, ALU.is_equal))
                for k in range(1, TOPK):
                    link(dve.scalar_tensor_tensor(emask[:, tt, :], iota[:, :], eidxf[:, tt, k:k + 1], emask[:, tt, :],
                                                  ALU.is_equal, ALU.add))
                link(dve.tensor_tensor(esel[:, tt, :], sc[:, tt, :], emask[:, tt, :], ALU.mult))
                link(dve.tensor_reduce(wsum[:, tt, 0:1], esel[:, tt, :], AX.X, ALU.add))
                link(dve.tensor_scalar(wsum[:, tt, 1:2], wsum[:, tt, 0:1], 1e-20, None, ALU.add))
                link(dve.reciprocal(wsum[:, tt, 2:3], wsum[:, tt, 1:2]))
                dve.tensor_scalar(comb[:, tt, :], esel[:, tt, :], wsum[:, tt, 2:3], SCALE, ALU.mult, ALU.mult) \
                   .then_inc(cmb, 1)

            def gate(n):
                dve.wait_ge(h3_mm, n + 1)
                if n >= 1:
                    dve.wait_ge(sw, n)
                else:
                    dve.wait_ge(silu, 1)
                s = rtmp[:, 2 + n % 2, :] if n >= 1 else rtmp[:, 0, :]
                if n >= 2:
                    dve.wait_ge(g_hi, n - 1)
                    dve.wait_ge(g_lo, n - 1)
                dve.tensor_tensor(rtmp[:, 4 + n % 2, :], h_ps[2 * (n % 2) + 1][:, :], s, ALU.mult).then_inc(gated, 1)

            def gate_lo(n):
                dve.wait_ge(g_hi, n + 1)
                dve.tensor_tensor(pT_flat[:, 2 + n % 2, 0:T], rtmp[:, 4 + n % 2, :], f(pT_flat[:, n % 2, 0:T]),
                                  ALU.subtract).then_inc(g_lo, 1)

            dve.wait_ge(d_gate, 48)
            route(0)
            gate(0)
            gate_lo(0)
            for tt in range(1, TT):
                route(tt)
            for n in range(1, NX):
                if n + 1 < NX:
                    weight_hi(n + 1)
                gate(n)
                gate_lo(n)
            dve.wait_ge(w2_mm, NX)
            dve.tensor_copy(prob[:, 1, :], acc_ps[1][:, :]).then_inc(fin[1], 1)

        @block.gpsimd
        def _(pool):
            links = [0]

            def link(ins):
                links[0] += 1
                ins.then_inc(chain_p, 1)
                pool.wait_ge(chain_p, links[0])

            pool.wait_ge(d_kv, 32)
            hd = DC // 2
            for b in range(B):
                rows = slice(b * LC, (b + 1) * LC)
                pool.tensor_tensor(kvr[:, rows, 0, :], kv[:, rows, :], kvtab[:, :, 0, :], ALU.mult)
                pool.tensor_tensor(kvr[:, rows, 1, 0:hd], kv[:, rows, hd:DC], kvtab[:, :, 1, 0:hd], ALU.mult)
                link(pool.tensor_tensor(kvr[:, rows, 1, hd:DC], kv[:, rows, 0:hd], kvtab[:, :, 1, hd:DC], ALU.mult))
            link(pool.tensor_tensor(kvr[:, :, 0, :], kvr[:, :, 0, :], kvr[:, :, 1, :], ALU.add))
            pool.tensor_copy(kvr[:, :, 1, :], kvr[:, :, 0, :]).then_inc(kv_roped, 1)

            def ropes(g, c):
                n = NCH * g + c
                pool.wait_ge(wk_out, USES * g + HG + 2 + NPG + 2 * c + 2)
                if g >= 1:
                    pool.wait_ge(qr_mm, NPG * (g - 1) + (1 if c == 0 else 2))
                if g == 1 and c == 0:
                    pool.wait_ge(rope_a, NCH)
                if g >= 1:
                    link(rope_half(pool, ALU, link, n, c, 0))
                rope_half(pool, ALU, link, n, c, 1).then_inc(rope_p, 1)
                pool.wait_ge(rope_p, n + 1)

            def weight_lo(n):
                pool.wait_ge(wx_hi, n + 1)
                if n >= SPL:
                    pool.wait_ge(w2_mm, n - SPL + 1)
                pool.tensor_tensor(w_v[:, n % SPL, 1, :], raw_v[:, n % RAW, :], f(w_v[:, n % SPL, 0, :]), ALU.subtract) \
                    .then_inc(wx_lo, 1)

            def weigh(n):
                pool.wait_ge(silu, n + 1)
                e = n - 1
                pool.wait_ge(d_cb[e % CBR], 16 * (e // CBR + 1))
                if n >= 3:
                    pool.wait_ge(gated, n - 1)
                pool.tensor_tensor(rtmp[:, 2 + n % 2, :], rtmp[:, n % 2, :], roped_flat[:, e % CBR, :], ALU.mult) \
                    .then_inc(sw, 1)

            pool.wait_ge(d_rope, 16)
            for g in range(NG):
                for c in range(NCH):
                    ropes(g, c)
            weight_lo(0)
            weight_lo(1)
            for n in range(1, NX):
                weigh(n)
                if n + 1 < NX:
                    weight_lo(n + 1)


def rope_tables(length, dim):
    inv = (np.float32(1.0) / np.float32(10000.0) ** (np.arange(0, dim, 2, dtype=np.float32) / np.float32(dim)))
    f = np.arange(length, dtype=np.float32)[:, None] * inv.astype(np.float32)[None, :]
    return np.repeat(np.sin(f), 2, axis=-1), np.repeat(np.cos(f), 2, axis=-1)


def kernel(x, ctx_512, L0_xattn_Wq, L0_xattn_w_kc_q, L0_xattn_w_kc_kv, L0_xattn_W_qr, L0_xattn_W_kr, L0_xattn_Wo,
           L0_ffn_gate_weight, L0_ffn_e_score_correction_bias, L0_ffn_w1, L0_ffn_w3, L0_ffn_w2, L0_ffn_ws1,
           L0_ffn_ws3, L0_ffn_ws2):
    import concourse.bacc as bacc
    from concourse.bass_utils import run_bass_kernel_spmd

    a = np.asarray
    c = np.ascontiguousarray
    f32 = np.float32
    x_l = c(a(x).reshape(TT, P, D).transpose(1, 0, 2))
    kv_l = c(a(ctx_512).reshape(B * LC, P, DC).transpose(1, 0, 2))
    w_attn = np.zeros((NG, P, WGRP), f32)
    wq = a(L0_xattn_Wq).reshape(NG, HG, K, D)
    w_attn[:, :, 0:HG * D] = wq.transpose(0, 2, 1, 3).reshape(NG, K, HG * D)
    w_attn[:, :, HG * D:WM] = a(L0_xattn_w_kc_q).reshape(NG, HG, K, CQ).transpose(0, 2, 1, 3).reshape(NG, K, HG * CQ)
    wqr, wkr = a(L0_xattn_W_qr), a(L0_xattn_W_kr)
    for g in range(NG):
        for m, (ch, j) in enumerate(COMBOS):
            for i in range(2):
                head = 2 * j + i
                lo, hi = max(ch * P, head * HALF), min((ch + 1) * P, (head + 1) * HALF)
                if lo >= hi:
                    continue
                for ab in range(2):
                    col = WM + (m * 2 + ab) * P + lo - ch * P
                    q0 = ab * HALF + lo - head * HALF
                    w_attn[g, i * R:(i + 1) * R, col:col + hi - lo] = wqr[g * HG + head, q0:q0 + hi - lo, :].T
        for j in range(NPG):
            for i in range(2):
                col = WM + NCO * 2 * P + j * P + i * DC
                w_attn[g, i * R:(i + 1) * R, col:col + DC] = wkr[g * HG + 2 * j + i].T
    o = WM + WG
    w_attn[:, :, o:o + HG * DC] = a(L0_xattn_w_kc_kv).reshape(NG, HG, K, DC).transpose(0, 2, 1, 3).reshape(NG, K, HG * DC)
    w_attn[:, :, o + HG * DC:] = a(L0_xattn_Wo).T.reshape(NG, HG, K, D).transpose(0, 2, 1, 3).reshape(NG, K, HG * D)
    gate_l = c(a(L0_ffn_gate_weight).T.reshape(ND, P, E).transpose(1, 0, 2))
    bias_l = c(np.broadcast_to(a(L0_ffn_e_score_correction_bias), (P, E)))
    w1 = np.concatenate([a(L0_ffn_ws1)[None], a(L0_ffn_w1)])
    w3 = np.concatenate([a(L0_ffn_ws3)[None], a(L0_ffn_w3)])
    w2 = np.concatenate([a(L0_ffn_ws2)[None], a(L0_ffn_w2)])
    w_exp = np.concatenate([w.transpose(0, 2, 1).reshape(NX, ND, P, I).transpose(0, 2, 1, 3).reshape(NX, P, ND * I)
                            for w in (w1, w3)] + [w2.transpose(0, 2, 1)], axis=2)

    sin_q, cos_q = rope_tables(S, CQ)
    rope_q = np.zeros((P, NCH, 4, S), f32)
    for ch in range(NCH):
        i = (ch * P + np.arange(P)) % HALF
        rope_q[:, ch, 0], rope_q[:, ch, 1] = cos_q.T[i], -sin_q.T[i]
        rope_q[:, ch, 2], rope_q[:, ch, 3] = cos_q.T[i + HALF], sin_q.T[i + HALF]
    sin_k, cos_k = rope_tables(L, DC)
    sign = np.where(np.arange(DC) < DC // 2, f32(-1), f32(1))
    rope_kv = c(np.stack([cos_k, sin_k * sign], 1).reshape(LC, P, 2, DC).transpose(1, 0, 2, 3).astype(f32))
    ident = np.eye(P, dtype=f32)
    iota = c(np.broadcast_to(np.arange(E, dtype=f32), (P, E)))

    nc = bacc.Bacc("TRN2", target_bir_lowering=False, num_devices=1)
    arrays = {"x": x_l, "ctx_kv": kv_l, "w_attn": w_attn, "w_gate": gate_l, "gate_bias": bias_l, "w_exp": c(w_exp),
              "rope_q": rope_q, "rope_kv": rope_kv, "ident": ident, "iota": iota}
    aps = [nc.dram_tensor(f"in_{n}", v.shape, mybir.dt.from_np(v.dtype), kind="ExternalInput").ap()
           for n, v in arrays.items()]
    c_dram = nc.dram_tensor("combine_scratch", (E, T), F32, kind="Internal").ap()
    out = nc.dram_tensor("out_T", (D, T), F32, kind="ExternalOutput").ap()
    build(nc, *aps, c_dram, out)
    r = run_bass_kernel_spmd(nc, [{f"in_{n}": v for n, v in arrays.items()}], core_ids=[0])
    return r.results[0]["out_T"].T.reshape(B, S, D)
```

```python
from contextlib import ExitStack

import numpy as np
import concourse.bass as bass
from concourse import mybir

ALU = mybir.AluOpType
ACT = mybir.ActivationFunctionType
AX = mybir.AxisListType
F32 = mybir.dt.float32
F32R = mybir.dt.float32r
U32 = mybir.dt.uint32

P = 128
B, S, D = 2, 256, 256
L, DC = 512, 64
H, K, R, CQ = 16, 128, 64, 192
T = B * S
TT = T // P
ND = D // P
LC = L // P
HALF = CQ // 2
E, G, GE, TOPG, TOPK, I = 32, 4, 8, 2, 4, 128
SCALE = 2.5
EPS = 1e-5

HG = 4
NG = H // HG
NCH = HG * HALF // P
NPG = HG // 2
NP = H // 2
COMBOS = ((0, 0), (1, 0), (1, 1), (2, 1))
NCO = len(COMBOS)
WM = HG * (D + CQ)
WG = NCO * 2 * P + NPG * P
WN = HG * (DC + D)
WGRP = WM + WG + WN
ORDER = ("M0", "M1", "M2", "G0", "G1", "M3", "A0", "B0", "A1", "B1", "N0", "N1",
         "A2", "B2", "R3", "P3")
USES = len(ORDER)
TILES = H * B * (S // P)
TPG = TILES // NG
WE = 2 * ND * I + D
NX = E + 1
RAW = 2 * WGRP // WE
SPL_M, SPL = 3, 5
AHEAD = 3
ROPE_V = 2
LOOK = 3
CB_PE = 2
CBR = 6


def build(nc, x, ctx_kv, w_attn, w_gate, gate_bias, w_exp, rope_q, rope_kv, ident_in, iota_in, c_dram, out):
    with ExitStack() as stack:
        def sb(name, shape, dt=F32):
            return stack.enter_context(nc.sbuf_tensor(name, shape, dt))

        def sem(name):
            return stack.enter_context(nc.semaphore(name))

        x_sb = sb("x_sb", [P, TT, D])
        xn = sb("xn", [P, TT, D])
        xnT = sb("xnT", [P, 2, ND, T], F32R)
        wring = sb("wring", [P, 2 * WGRP])
        msplit = sb("msplit", [P, SPL_M * 2 * WE], F32R)
        gmat = sb("gmat", [P, 2, NCO, P])
        nmat = sb("nmat", [P, NP, D])
        rope = sb("rope", [P, NCH, 4, S])
        abuf = sb("abuf", [P, 2, 2, T])
        rtmp = sb("rtmp", [P, 6, T])
        roped = sb("roped", [P, NCH, 2, T])
        qsp = sb("qsp", [P, 4, 2, T], F32R)
        kdup = sb("kdup", [P, 2, B * L], F32R)
        kvs = sb("kvs", [P, B * LC, P], F32R)
        prob = sb("prob", [P, 3, L])
        pT = sb("pT", [P, 2, 2, LC, S], F32R)
        ctmp = sb("ctmp", [P, 2, S])
        ctT = sb("ctT", [P, NP, T])
        kv = sb("kv", [P, B * LC, DC])
        kvr = sb("kvr", [P, B * LC, 2, DC])
        kvtab = sb("kvtab", [P, LC, 2, DC])
        ident = sb("ident", [P, P])
        iota = sb("iota", [P, E])
        gateT = sb("gateT", [P, ND, E])
        bias = sb("bias", [P, E])
        stat = sb("stat", [P, 2 * TT, 6])
        mv = sb("mv", [P, 2 * TT, 2])
        std = sb("std", [P, 2 * TT, 1])
        rstd = sb("rstd", [P, 2 * TT, 1])
        nmax = sb("nmax", [P, TILES])
        psum_e = sb("psum_e", [P, TILES])
        rsum = sb("rsum", [P, TILES])
        sc = sb("sc", [P, TT, E])
        sfc = sb("sfc", [P, TT, E])
        g8 = sb("g8", [P, TT, G, 8])
        gs = sb("gs", [P, TT, 8])
        gtop = sb("gtop", [P, TT, 8])
        gidx = sb("gidx", [P, TT, 8], U32)
        gidxf = sb("gidxf", [P, TT, 8])
        gmask = sb("gmask", [P, TT, G])
        masked = sb("masked", [P, TT, E])
        etop = sb("etop", [P, TT, 8])
        eidx = sb("eidx", [P, TT, 8], U32)
        eidxf = sb("eidxf", [P, TT, 8])
        emask = sb("emask", [P, TT, E])
        esel = sb("esel", [P, TT, E])
        wsum = sb("wsum", [P, TT, 3])
        comb = sb("comb", [P, TT, E])
        combT = prob[0:E, 2, :]
        epsc = sb("epsc", [P, 1])
        warm = sb("warm", [P, 2])

        bank = [stack.enter_context(nc.psum_tensor(f"bank{i}", [P, 512], F32)) for i in range(8)]
        work = bank[0:2]
        s_ps = bank[2:5]
        t_ps = bank[5:7]
        pv_ps = bank[7]
        h_ps = bank[0:4]
        r_ps = bank[3:5]
        cb_ps = bank[4]
        o_ps = bank[0:2]
        acc_ps = bank[5:7]
        g_ps = bank[7]

        def half_of(g):
            return (g % 2) * WGRP

        def wq(g, i, dc):
            a = half_of(g) + i * D + dc * P
            return wring[:, a:a + P]

        def wkcq(g, i):
            a = half_of(g) + HG * D + i * CQ
            return wring[:, a:a + CQ]

        def wqrT(g, m, ab):
            a = half_of(g) + WM + (m * 2 + ab) * P
            return wring[:, a:a + P]

        def wkrT(g, j):
            a = half_of(g) + WM + NCO * 2 * P + j * P
            return wring[:, a:a + P]

        def wkv(g, i):
            a = half_of(g) + WM + WG + i * DC
            return wring[:, a:a + DC]

        def woT(g, i):
            a = half_of(g) + WM + WG + HG * DC + i * D
            return wring[:, a:a + D]

        qsp_flat = qsp[:, :, :, :].rearrange("p a b t -> p (a b t)")
        m_v = msplit[:, 0:2 * ND * 2 * HG * HALF].rearrange("p (s d a n) -> p s d a n", s=2, d=ND, a=2)
        w_slots = [t.rearrange("p (s n) -> p s n", s=2) for t in
                   [msplit[:, r * 2 * WE:(r + 1) * 2 * WE] for r in range(SPL_M)] +
                   [qsp_flat[:, r * 2 * WE:(r + 1) * 2 * WE] for r in range(SPL - SPL_M)]]
        raw_v = wring[:, 0:RAW * WE].rearrange("p (r n) -> p r n", r=RAW)
        roped_flat = roped[:, :, :, :].rearrange("p c a t -> p (c a) t")
        pT_flat = pT[:, :, :, :, :].rearrange("p s b c q -> p (s b) (c q)")
        eq_v = prob[:, 0, :]

        probs = [prob[:, 0, :], prob[:, 1, :], prob[:, 2, :], xn[:, 0:2, :].rearrange("p t d -> p (t d)")]
        xT_f = abuf[:, :, :, 0:P]
        xn_out = [prob[:, 0, :], prob[:, 1, :]]

        def f(ap):
            return ap.bitcast(F32)

        d_x = sem("d_x"); d_kv = sem("d_kv"); d_const = sem("d_const"); d_rope = sem("d_rope"); d_gate = sem("d_gate")
        d_wm = [sem(f"d_wm{i}") for i in range(2)]
        d_wg = [sem(f"d_wg{i}") for i in range(2)]
        d_wn = [sem(f"d_wn{i}") for i in range(2)]
        d_raw = [sem(f"d_raw{i}") for i in range(RAW)]
        d_ct = sem("d_ct"); d_cb = [sem(f"d_cb{i}") for i in range(CBR)]
        d_out = sem("d_out")
        chain_v = sem("chain_v")
        chain_p = sem("chain_p")
        ln_std = sem("ln_std"); ln_mv = sem("ln_mv"); ln_xn = sem("ln_xn")
        kv_roped = sem("kv_roped"); kv_split = sem("kv_split")
        xT_mm = sem("xT_mm"); xT_hi = sem("xT_hi"); xT_lo = sem("xT_lo")
        kT_mm = sem("kT_mm"); kT_hi = sem("kT_hi"); kT_lo = sem("kT_lo")
        wk_full = sem("wk_full"); wk_out = sem("wk_out"); m_lo = sem("m_lo")
        rope_a = sem("rope_a"); rope_p = sem("rope_p")
        q_lo = sem("q_lo")
        s_mm = sem("s_mm"); s_max = sem("s_max"); s_exp = sem("s_exp"); s_inv = sem("s_inv"); s_norm = sem("s_norm")
        t_mm = sem("t_mm"); t_hi = sem("t_hi"); t_lo = sem("t_lo")
        pv_mm = sem("pv_mm"); c_half = sem("c_half"); c_sum = sem("c_sum")
        o_mm = sem("o_mm"); x1_done = sem("x1_done"); x1_stat = sem("x1_stat"); x2_std = sem("x2_std"); x2_mv = sem("x2_mv"); x2_n = sem("x2_n")
        y_mm = sem("y_mm"); y_f = sem("y_f"); y_hi = sem("y_hi"); y_lo = sem("y_lo")
        lg_mm = sem("lg_mm"); lg_sc = sem("lg_sc"); cmb = sem("cmb"); ct_mm = sem("ct_mm"); ct_sb = sem("ct_sb")
        cb_mm = sem("cb_mm"); cb_sb = sem("cb_sb"); wx_hi = sem("wx_hi"); wx_lo = sem("wx_lo")
        h1_mm = sem("h1_mm"); h3_mm = sem("h3_mm"); silu = sem("silu"); sw = sem("sw"); gated = sem("gated")
        g_hi = sem("g_hi"); g_lo = sem("g_lo"); w2_mm = sem("w2_mm"); fin = [sem(f"fin{i}") for i in range(ND)]

        STEADY = {0: "M0 M1", 1: "M2 G0", 2: "G1 M3", 3: "A0", 4: "B0", 5: "A1", 6: "B1", 7: "N0 N1", 8: "A2", 9: "B2",
                  10: "R0 R1", 11: "R2", 12: "R3", 13: "P0", 14: "P1", 15: "P2 P3"}
        PLAN = [
            {0: "-P0 -P1", 1: "-P2 -P3", 2: "M0 M1", 3: "M2 G0", 4: "G1 M3", 5: "A0", 6: "B0", 7: "A1", 8: "B1 N0 N1",
             9: "A2", 10: "B2", 11: "R0 R1", 12: "R2 R3", 13: "P0", 14: "P1 P2", 15: "P3"},
            STEADY,
            STEADY,
            {2: "O0", 4: "O1", 6: "O2", 8: "O3", 10: "O4", 11: "O5", 14: "O6"},
        ]

        def steps(t):
            g = t // TPG
            for s in PLAN[g].get(t % TPG, "").split():
                yield (g, s[1], int(s[2])) if s[0] == "-" else (g + 1, s[0], int(s[1]))

        PROLOGUE = [(0, s[0], int(s[1])) for s in "A0 B0 A1 B1 N0 N1 A2 B2 R0 R1 R2 R3".split()]

        def use(g, kind, i):
            return USES * g + ORDER.index(f"{kind}{i}")

        N_DONE = [use(g, "N", 1) + 1 for g in range(NG)]
        Q_DONE = [use(g, "B", 2) + 1 for g in range(NG)]

        block = stack.enter_context(nc.Block())

        def rope_half(eng, link, n, c, ab):
            own, other = abuf[:, n % 2, ab, :], abuf[:, n % 2, 1 - ab, :]
            cos = rope[:, c, 2 * ab, :].unsqueeze(1).to_broadcast([P, B, S])
            sin = rope[:, c, 2 * ab + 1, :].unsqueeze(1).to_broadcast([P, B, S])
            t0, t1 = rtmp[:, 2 * ab, :], rtmp[:, 2 * ab + 1, :]
            eng.tensor_tensor(t0.rearrange("p (b s) -> p b s", b=B), own.rearrange("p (b s) -> p b s", b=B), cos, ALU.mult)
            link(eng.tensor_tensor(t1.rearrange("p (b s) -> p b s", b=B), other.rearrange("p (b s) -> p b s", b=B), sin,
                                   ALU.mult))
            return eng.tensor_tensor(roped[:, c, ab, :], t0, t1, ALU.add)

        @block.sync
        def _(sp):
            sp.dma_start(x_sb[:, :, :], x).then_inc(d_x, 16)
            sp.dma_start(ident[:, :], ident_in).then_inc(d_const, 16)

            def load_group(g, part):
                a, n, s = {"m": (0, WM, d_wm), "g": (WM, WG, d_wg), "n": (WM + WG, WN, d_wn)}[part]
                sp.dma_start(wring[:, half_of(g) + a:half_of(g) + a + n], w_attn[g, :, a:a + n]).then_inc(s[g % 2], 16)

            load_group(0, "m")
            sp.dma_start(kv[:, :, :], ctx_kv).then_inc(d_kv, 16)
            sp.dma_start(kvtab[:, :, :, :], rope_kv).then_inc(d_kv, 16)
            sp.dma_start(rope[:, :, :, :], rope_q).then_inc(d_rope, 16)
            load_group(0, "g")
            load_group(0, "n")
            for part in "mgn":
                load_group(1, part)
            sp.dma_start(gateT[:, :, :], w_gate).then_inc(d_gate, 16)
            sp.dma_start(bias[:, :], gate_bias).then_inc(d_gate, 16)
            sp.dma_start(iota[:, :], iota_in).then_inc(d_gate, 16)
            for g in range(2, NG):
                sp.wait_ge(wk_full, N_DONE[g - 2])
                for part in "mgn":
                    load_group(g, part)
            def load_cb(e):
                if e < E:
                    sp.wait_ge(sw, e - CBR + 1)
                    sp.dma_start(roped_flat[:, e % CBR, :], c_dram[e:e + 1, :].to_broadcast([P, T])) \
                      .then_inc(d_cb[e % CBR], 16)

            for n in range(NX):
                if n < RAW:
                    last = NG - 2 if (n + 1) * WE <= WGRP else NG - 1
                    sp.wait_ge(wk_full, N_DONE[last])
                else:
                    sp.wait_ge(wx_lo, n - RAW + 1)
                sp.dma_start(raw_v[:, n % RAW, :], w_exp[n]).then_inc(d_raw[n % RAW], 16)
                if n == RAW - 1:
                    sp.wait_ge(ct_sb, 1)
                    sp.dma_start(c_dram, combT).then_inc(d_ct, 16)
                    sp.wait_ge(d_ct, 16)
                    for e in range(CB_PE, CBR):
                        sp.dma_start(roped_flat[:, e, :], c_dram[e:e + 1, :].to_broadcast([P, T])).then_inc(d_cb[e], 16)
                if n >= RAW:
                    load_cb(n - RAW + CBR)
            for e in range(NX - RAW + CBR, E):
                load_cb(e)
            for dc in range(ND):
                sp.wait_ge(fin[dc], 1)
                sp.dma_start(out[dc * P:(dc + 1) * P, :], xn_out[dc]).then_inc(d_out, 16)
            sp.wait_ge(d_out, 16 * ND)

        @block.tensor
        def _(pe):
            def split3(out_ap, a_hi, a_lo, b_hi, b_lo, first, last):
                pe.matmul(out_ap, a_hi, b_hi, start=first, stop=False)
                pe.matmul(out_ap, a_hi, b_lo, start=False, stop=False)
                return pe.matmul(out_ap, a_lo, b_hi, start=False, stop=last)

            def bank_free(u):
                if u >= 2:
                    g, k = divmod(u - 2, USES)
                    if ORDER[k][0] == "M":
                        pe.wait_ge(m_lo, HG * g + int(ORDER[k][1]) + 1)
                    elif ORDER[k][0] in "RP":
                        pe.wait_ge(q_lo, NPG * g + "RP".index(ORDER[k][0]) + 1)
                    else:
                        pe.wait_ge(wk_out, u - 1)

            def step(g, kind, i):
                if kind in "MGABN":
                    u = use(g, kind, i)
                    bank_free(u)
                if kind == "M":
                    pe.wait_ge(d_wm[g % 2], 16 * (g // 2 + 1))
                    for dc in range(ND):
                        mm = pe.matmul(work[u % 2][:, dc * CQ:(dc + 1) * CQ], wq(g, i, dc), wkcq(g, i),
                                       start=True, stop=True)
                    mm.then_inc(wk_full, 1)
                elif kind == "G":
                    pe.wait_ge(d_wg[g % 2], 16 * (g // 2 + 1))
                    for m, (_, j) in enumerate(COMBOS):
                        mm = pe.matmul(work[u % 2][:, m * P:(m + 1) * P], wqrT(g, m, i), wkrT(g, j),
                                       start=True, stop=True)
                    mm.then_inc(wk_full, 1)
                elif kind == "N":
                    pe.wait_ge(d_wn[g % 2], 16 * (g // 2 + 1))
                    for k in range(2):
                        mm = pe.matmul(work[u % 2][k * DC:(k + 1) * DC, 0:D], wkv(g, 2 * i + k), woT(g, 2 * i + k),
                                       start=True, stop=True)
                    mm.then_inc(wk_full, 1)
                elif kind in "AB":
                    ab = "AB".index(kind)
                    pe.wait_ge(m_lo, HG * g + i + 2)
                    if g == 0:
                        pe.wait_ge(xT_lo, ND)
                    for dc in range(ND):
                        cols = slice(i * P, (i + 1) * P)
                        mm = split3(work[u % 2][:, :], m_v[:, 0, dc, ab, cols], m_v[:, 1, dc, ab, cols],
                                    xnT[:, 0, dc, :], xnT[:, 1, dc, :], dc == 0, dc == ND - 1)
                    mm.then_inc(wk_full, 1)
                elif kind in "RP":
                    j = "RP".index(kind)
                    c, ab = j + i // 2, i % 2
                    u = use(g, kind, 3)
                    if i == 0:
                        bank_free(u)
                        pe.wait_ge(wk_out, use(g, "G", 1) + 1)
                    if ab == 0:
                        pe.wait_ge(rope_p, NCH * g + c + 1)
                        if g < ROPE_V:
                            pe.wait_ge(rope_a, NCH * g + c + 1)
                    mm = pe.matmul(work[u % 2][:, :], gmat[:, ab, COMBOS.index((c, j)), :], roped[:, c, ab, :],
                                   start=(i == 0), stop=(i == 3))
                    if i == 3:
                        mm.then_inc(wk_full, 1)
                else:
                    pe.wait_ge(wk_out, USES * NG)
                    pe.wait_ge(c_sum, 4 * i + 4)
                    for tt in range(TT):
                        mm = pe.matmul(o_ps[tt // 2][:, (tt % 2) * D:(tt % 2 + 1) * D], ctT[:, i, tt * P:(tt + 1) * P],
                                       nmat[:, i, :], start=(i == 0 and tt % 2 == 0), stop=(i == NP - 1 and tt % 2 == 1),
                                       skip_group_check=True)
                    if i == NP - 1:
                        mm.then_inc(o_mm, 1)

            def scores(t):
                h, b, st = t // 4, (t // 2) % 2, t % 2
                pe.wait_ge(q_lo, h // 2 + 1)
                if t == 0:
                    pe.wait_ge(kT_lo, 2)
                if t >= 3:
                    pe.wait_ge(s_exp, t - 2)
                q = qsp[:, (h // 2) % 4, h % 2, b * S + st * P:b * S + (st + 1) * P]
                pe.matmul(s_ps[t % 3][:, :], q, kdup[:, 0, b * L:(b + 1) * L], start=True, stop=False)
                pe.matmul(s_ps[t % 3][:, :], q, kdup[:, 1, b * L:(b + 1) * L], start=False, stop=True) \
                  .then_inc(s_mm, 1)

            def transposes(t):
                pe.wait_ge(s_norm, t + 1)
                if t >= 2:
                    pe.wait_ge(t_lo, t - 1)
                for lc in range(LC):
                    mm = pe.transpose(t_ps[t % 2][:, lc * P:(lc + 1) * P], probs[t % 4][:, lc * P:(lc + 1) * P],
                                      ident[:, :])
                mm.then_inc(t_mm, 1)

            def attend(hb):
                b = hb % 2
                pe.wait_ge(t_lo, 2 * hb + 2)
                if hb == 0:
                    pe.wait_ge(kv_split, 2)
                if hb >= 1:
                    pe.wait_ge(c_sum, hb)
                for n in range(2 * LC):
                    lc, hl = n // 2, n % 2
                    mm = pe.matmul(pv_ps[:, b * S:(b + 1) * S], kvs[:, b * LC + lc, :], pT[:, hl, hb % 2, lc, :],
                                   start=(n == 0), stop=(n == 2 * LC - 1))
                mm.then_inc(pv_mm, 1)

            pe.wait_ge(d_const, 16)
            for i in range(3):
                step(0, "M", i)
            for tt in range(TT):
                pe.wait_ge(ln_xn, tt + 1)
                for dc in range(ND):
                    mm = pe.transpose(t_ps[dc][:, tt * P:(tt + 1) * P], xn[:, tt, dc * P:(dc + 1) * P], ident[:, :])
            mm.then_inc(xT_mm, 1)
            for i in range(2):
                step(0, "G", i)
            step(0, "M", 3)
            step(*PROLOGUE[0])
            pe.wait_ge(kv_roped, 1)
            for n in range(B * LC):
                mm = pe.transpose(s_ps[n // LC][:, (n % LC) * P:(n % LC + 1) * P],
                                  kvr[:, n, :, :].rearrange("p a c -> p (a c)"), ident[:, :])
            mm.then_inc(kT_mm, 1)
            for s in PROLOGUE[1:]:
                step(*s)
            pe.wait_ge(kT_lo, 2)
            for t in range(LOOK):
                scores(t)
            for t in range(TILES):
                if t + LOOK < TILES:
                    scores(t + LOOK)
                for s in steps(t):
                    step(*s)
                transposes(t)
                if t % 2 == 1 and t >= 3:
                    attend((t - 3) // 2)
            attend(TILES // 2 - 1)

            step(NG, "O", NP - 1)

            def rows_T(tt):
                pe.wait_ge(x2_n, tt + 1)
                if tt >= 2:
                    pe.wait_ge(y_lo, tt - 1)
                for dc in range(ND):
                    mm = pe.transpose(r_ps[tt % 2][:, dc * P:(dc + 1) * P], xn[:, tt, dc * P:(dc + 1) * P], ident[:, :])
                mm.then_inc(y_mm, 1)

            def seed(tt):
                pe.wait_ge(x1_done, tt + 1)
                for dc in range(ND):
                    pe.matmul(acc_ps[dc][:, tt * P:(tt + 1) * P], x_sb[:, tt, dc * P:(dc + 1) * P], ident[:, :],
                              start=(tt == 0), stop=False, skip_group_check=True)

            def logits(tt):
                pe.wait_ge(y_f, tt + 1)
                for dc in range(ND):
                    mm = pe.matmul(g_ps[:, tt * E:(tt + 1) * E], xT_f[:, tt % 2, dc, :], gateT[:, dc, :],
                                   start=(dc == 0), stop=(dc == ND - 1))
                mm.then_inc(lg_mm, 1)

            def expert_in(n):
                if n >= 2:
                    pe.wait_ge(gated, n - 1)
                pe.wait_ge(wx_lo, n + 1)
                for w, signal in ((0, h1_mm), (1, h3_mm)):
                    for dc in range(ND):
                        a = (w * ND + dc) * I
                        mm = split3(h_ps[2 * (n % 2) + w][:, :], w_slots[n % SPL][:, 0, a:a + I], w_slots[n % SPL][:, 1, a:a + I],
                                    xnT[:, 0, dc, :], xnT[:, 1, dc, :], dc == 0, dc == ND - 1)
                    mm.then_inc(signal, 1)

            def expert_out(n):
                pe.wait_ge(g_lo, n + 1)
                for dc in range(ND):
                    a = 2 * ND * I + dc * P
                    w_hi, w_lo = w_slots[n % SPL][:, 0, a:a + P], w_slots[n % SPL][:, 1, a:a + P]
                    gh, gl = pT_flat[:, n % 2, 0:T], pT_flat[:, 2 + n % 2, 0:T]
                    for k, (wp, gp) in enumerate(((w_hi, gh), (w_hi, gl), (w_lo, gh))):
                        mm = pe.matmul(acc_ps[dc][:, :], wp, gp, start=False, stop=(n == NX - 1 and k == 2),
                                       skip_group_check=True)
                mm.then_inc(w2_mm, 1)

            pe.wait_ge(d_gate, 48)
            for tt in range(TT):
                seed(tt)
                rows_T(tt)
                if tt >= 1:
                    logits(tt - 1)
            logits(TT - 1)
            pe.wait_ge(y_lo, TT)
            expert_in(0)
            expert_in(1)
            pe.wait_ge(cmb, 1)
            pe.wait_ge(lg_sc, 1)
            for tt in range(TT):
                mm = pe.transpose(g_ps[0:E, tt * P:(tt + 1) * P], comb[:, tt, :], ident[:, :])
            mm.then_inc(ct_mm, 1)
            pe.wait_ge(ct_sb, 1)
            for e in range(CB_PE):
                if e >= 1:
                    pe.wait_ge(cb_sb, e)
                pe.matmul(cb_ps[:, :], ident[0:E, e:e + 1].to_broadcast([E, P]), combT, start=True, stop=True) \
                  .then_inc(cb_mm, 1)
            expert_out(0)
            for n in range(1, NX):
                if n + 1 < NX:
                    expert_in(n + 1)
                expert_out(n)

        @block.scalar
        def _(act):
            act.wait_ge(ln_mv, TT)
            act.activation(std[:, 0:TT, 0], mv[:, 0:TT, 1], ACT.Sqrt, bias=epsc[:, :]).then_inc(ln_std, 1)
            act.activation(warm[:, 0:1], epsc[:, :], ACT.Exp)

            def step(g, kind, i):
                if kind in "MGABN":
                    u = use(g, kind, i)
                    act.wait_ge(wk_full, u + 1)
                if kind == "M":
                    if g >= 1:
                        act.wait_ge(wk_full, Q_DONE[g - 1])
                    act.copy(m_v[:, 0, :, :, i * HALF:(i + 1) * HALF],
                             work[u % 2][:, 0:ND * CQ].rearrange("p (d a n) -> p d a n", d=ND, a=2)).then_inc(wk_out, 1)
                elif kind == "G":
                    if g >= 1:
                        act.wait_ge(wk_full, use(g - 1, "P", 3) + 1)
                    act.copy(gmat[:, i, :, :].rearrange("p m n -> p (m n)"), work[u % 2][:, :]).then_inc(wk_out, 1)
                elif kind == "N":
                    act.copy(nmat[:, NPG * g + i, :], work[u % 2][:, 0:D]).then_inc(wk_out, 1)
                elif kind in "AB":
                    n = NCH * g + i
                    if n >= 2:
                        act.wait_ge(rope_p, n - 1)
                        if (n - 2) // NCH < ROPE_V:
                            act.wait_ge(rope_a, n - 1)
                    act.copy(abuf[:, n % 2, "AB".index(kind), :], work[u % 2][:, :]).then_inc(wk_out, 1)
                elif kind in "RP" and i == 3:
                    p = NPG * g + "RP".index(kind)
                    u = use(g, kind, 3)
                    act.wait_ge(wk_full, u + 1)
                    if p >= 4:
                        act.wait_ge(s_mm, 8 * (p - 3))
                    act.copy(qsp[0:R, p % 4, 0, :], work[u % 2][0:R, :])
                    act.copy(qsp[R:P, p % 4, 1, :], work[u % 2][R:P, :]).then_inc(wk_out, 1)

            def exps(t):
                act.wait_ge(s_max, t + 1)
                if t >= 4:
                    act.wait_ge(t_mm, t - 3)
                act.activation(probs[t % 4], s_ps[t % 3][:, :], ACT.Exp, bias=nmax[:, t:t + 1],
                               accum_out=psum_e[:, t:t + 1]).then_inc(s_exp, 1)

            def prob_hi(t):
                hb = t // 2
                act.wait_ge(t_mm, t + 1)
                if hb >= 2:
                    act.wait_ge(pv_mm, hb - 1)
                act.copy(pT[:, 0, hb % 2, :, (t % 2) * P:(t % 2 + 1) * P],
                         t_ps[t % 2][:, :].rearrange("p (c q) -> p c q", c=LC)).then_inc(t_hi, 1)

            def ctx_half(hb):
                h, b = divmod(hb, 2)
                act.wait_ge(pv_mm, hb + 1)
                if hb >= 2:
                    act.wait_ge(c_sum, hb - 1)
                dst, src = (0, DC) if h % 2 == 0 else (DC, 0)
                act.copy(ctmp[dst:dst + DC, hb % 2, :], pv_ps[src:src + DC, b * S:(b + 1) * S]).then_inc(c_half, 1)

            for i in range(3):
                step(0, "M", i)
            act.wait_ge(xT_mm, 1)
            for dc in range(ND):
                act.copy(xnT[:, 0, dc, :], t_ps[dc][:, :]).then_inc(xT_hi, 1)
            for i in range(2):
                step(0, "G", i)
            step(0, "M", 3)
            step(*PROLOGUE[0])
            act.wait_ge(kT_mm, 1)
            for n in range(2):
                act.copy(kdup[:, 0, n * L:(n + 1) * L], s_ps[n][:, :]).then_inc(kT_hi, 1)
            for s in PROLOGUE[1:]:
                step(*s)
            for t in range(LOOK):
                exps(t)
            for t in range(TILES):
                if t + LOOK < TILES:
                    exps(t + LOOK)
                for s in steps(t):
                    step(*s)
                prob_hi(t)
                if t % 2 == 0 and t >= 4:
                    ctx_half((t - 4) // 2)
            ctx_half(TILES // 2 - 2)
            ctx_half(TILES // 2 - 1)

            act.wait_ge(x2_mv, TT)
            act.activation(std[:, TT:2 * TT, 0], mv[:, TT:2 * TT, 1], ACT.Sqrt, bias=epsc[:, :]).then_inc(x2_std, 1)
            act.activation(warm[:, 1:2], epsc[:, :], ACT.Sigmoid)
            for tt in range(TT):
                act.wait_ge(y_mm, tt + 1)
                if tt >= 2:
                    act.wait_ge(lg_mm, tt - 1)
                ps = r_ps[tt % 2][:, 0:ND * P].rearrange("p (d q) -> p d q", d=ND)
                act.copy(xT_f[:, tt % 2, :, :], ps).then_inc(y_f, 1)
                act.copy(xnT[:, 0, :, tt * P:(tt + 1) * P], ps).then_inc(y_hi, 1)
            act.wait_ge(lg_mm, TT)
            act.activation(sc[:, :, :].rearrange("p t e -> p (t e)"), g_ps[:, 0:TT * E], ACT.Sigmoid).then_inc(lg_sc, 1)

            def silus(n):
                act.wait_ge(h1_mm, n + 1)
                if n >= 2:
                    act.wait_ge(sw, n - 2)
                    act.wait_ge(gated, n - 1)
                act.activation(rtmp[:, n % 2, :], h_ps[2 * (n % 2)][:, :], ACT.Silu).then_inc(silu, 1)

            def gate_hi(n):
                act.wait_ge(gated, n + 1)
                if n >= 2:
                    act.wait_ge(w2_mm, n - 1)
                act.copy(pT_flat[:, n % 2, 0:T], rtmp[:, 4 + n % 2, :]).then_inc(g_hi, 1)

            silus(0)
            silus(1)
            act.wait_ge(ct_mm, 1)
            act.copy(combT, g_ps[0:E, :]).then_inc(ct_sb, 1)
            for e in range(CB_PE):
                act.wait_ge(cb_mm, e + 1)
                act.copy(roped_flat[:, e, :], cb_ps[:, :]).then_inc(cb_sb, 1)
            gate_hi(0)
            gate_hi(1)
            for n in range(2, NX):
                silus(n)
                gate_hi(n)
            act.wait_ge(w2_mm, NX)
            act.copy(prob[:, 0, :], acc_ps[0][:, :]).then_inc(fin[0], 1)

        @block.vector
        def _(dve):
            links = [0]

            def link(ins):
                links[0] += 1
                ins.then_inc(chain_v, 1)
                dve.wait_ge(chain_v, links[0])

            def norm_rows(o, got, signal):
                dve.wait_ge(got, 1)
                link(dve.reciprocal(rstd[:, o:o + TT, 0], std[:, o:o + TT, 0]))
                for tt in range(TT):
                    dve.tensor_scalar(xn[:, tt, :], x_sb[:, tt, :], mv[:, o + tt, 0:1], rstd[:, o + tt, :],
                                      ALU.subtract, ALU.mult).then_inc(signal, 1)

            dve.memset(gs[:, :, :], -3.0e38)
            link(dve.memset(epsc[:, :], EPS))
            dve.wait_ge(d_x, 16)
            for tt in range(TT):
                last = dve.bn_stats(stat[:, tt, :], x_sb[:, tt, :])
            link(last)
            for tt in range(TT):
                dve.bn_aggr(mv[:, tt, :], stat[:, tt, :]).then_inc(ln_mv, 1)
            norm_rows(0, ln_std, ln_xn)

            def step(g, kind, i):
                if kind == "M":
                    u = use(g, kind, i)
                    dve.wait_ge(wk_out, u + 1)
                    dve.tensor_tensor(m_v[:, 1, :, :, i * HALF:(i + 1) * HALF],
                                      work[u % 2][:, 0:ND * CQ].rearrange("p (d a n) -> p d a n", d=ND, a=2),
                                      f(m_v[:, 0, :, :, i * HALF:(i + 1) * HALF]), ALU.subtract).then_inc(m_lo, 1)
                elif kind == "B" and g < ROPE_V:
                    n = NCH * g + i
                    dve.wait_ge(wk_out, use(g, "B", i) + 1)
                    if g >= 1:
                        dve.wait_ge(wk_full, use(g - 1, "RPP"[i], 3) + 1)
                    rope_half(dve, link, n, i, 0).then_inc(rope_a, 1)
                    dve.wait_ge(rope_a, n + 1)
                elif kind in "RP" and i == 3:
                    p = NPG * g + "RP".index(kind)
                    u = use(g, kind, 3)
                    dve.wait_ge(wk_out, u + 1)
                    dve.tensor_tensor(qsp[R:P, p % 4, 0, :], work[u % 2][0:R, :], f(qsp[0:R, p % 4, 0, :]), ALU.subtract)
                    dve.tensor_tensor(qsp[0:R, p % 4, 1, :], work[u % 2][R:P, :], f(qsp[R:P, p % 4, 1, :]), ALU.subtract) \
                       .then_inc(q_lo, 1)

            def row_max(t):
                dve.wait_ge(s_mm, t + 1)
                dve.tensor_reduce(nmax[:, t:t + 1], s_ps[t % 3][:, :], AX.X, ALU.max, negate=True).then_inc(s_max, 1)

            def inverse(t):
                dve.wait_ge(s_exp, t + 1)
                dve.reciprocal(rsum[:, t:t + 1], psum_e[:, t:t + 1]).then_inc(s_inv, 1)

            def normalise(t):
                dve.wait_ge(s_inv, t + 1)
                dve.tensor_scalar(probs[t % 4], probs[t % 4], rsum[:, t:t + 1], None, ALU.mult).then_inc(s_norm, 1)

            def prob_lo(t):
                hb, q = t // 2, slice((t % 2) * P, (t % 2 + 1) * P)
                dve.wait_ge(t_hi, t + 1)
                dve.tensor_tensor(pT[:, 1, hb % 2, :, q], t_ps[t % 2][:, :].rearrange("p (c q) -> p c q", c=LC),
                                  f(pT[:, 0, hb % 2, :, q]), ALU.subtract).then_inc(t_lo, 1)

            def ctx_sum(hb):
                h, b = divmod(hb, 2)
                dve.wait_ge(c_half, hb + 1)
                r = (h % 2) * DC
                dve.tensor_tensor(ctT[r:r + DC, h // 2, b * S:(b + 1) * S], pv_ps[r:r + DC, b * S:(b + 1) * S],
                                  ctmp[r:r + DC, hb % 2, :], ALU.add).then_inc(c_sum, 1)

            for i in range(3):
                step(0, "M", i)
            for dc in range(ND):
                dve.wait_ge(xT_hi, dc + 1)
                dve.tensor_tensor(xnT[:, 1, dc, :], t_ps[dc][:, :], f(xnT[:, 0, dc, :]), ALU.subtract).then_inc(xT_lo, 1)
            step(0, "M", 3)
            dve.wait_ge(kv_roped, 1)
            dve.tensor_copy(kvs[:, :, 0:DC], kvr[:, :, 0, :]).then_inc(kv_split, 1)
            dve.wait_ge(kv_split, 1)
            dve.tensor_tensor(kvs[:, :, DC:P], kvr[:, :, 0, :], f(kvs[:, :, 0:DC]), ALU.subtract).then_inc(kv_split, 1)
            dve.wait_ge(d_rope, 16)
            step(*PROLOGUE[0])
            for n in range(2):
                dve.wait_ge(kT_hi, n + 1)
                dve.tensor_tensor(kdup[:, 1, n * L:(n + 1) * L], s_ps[n][:, :], f(kdup[:, 0, n * L:(n + 1) * L]),
                                  ALU.subtract).then_inc(kT_lo, 1)
            for s in PROLOGUE[1:]:
                step(*s)
            for t in range(LOOK):
                row_max(t)
            inverse(0)
            normalise(0)
            for t in range(TILES):
                if t + 1 < TILES:
                    inverse(t + 1)
                if t + LOOK < TILES:
                    row_max(t + LOOK)
                if t + 1 < TILES:
                    normalise(t + 1)
                if t >= 1:
                    prob_lo(t - 1)
                for s in steps(t):
                    step(*s)
                if t % 2 == 0 and t >= 4:
                    ctx_sum((t - 4) // 2)
            prob_lo(TILES - 1)
            ctx_sum(TILES // 2 - 2)
            ctx_sum(TILES // 2 - 1)

            def weight_hi(n):
                dve.wait_ge(d_raw[n % RAW], 16 * (n // RAW + 1))
                if n >= SPL:
                    dve.wait_ge(w2_mm, n - SPL + 1)
                dve.tensor_copy(w_slots[n % SPL][:, 0, :], raw_v[:, n % RAW, :]).then_inc(wx_hi, 1)

            for tt in range(TT):
                if tt == 0:
                    dve.wait_ge(o_mm, 1)
                dve.tensor_tensor(x_sb[:, tt, :], o_ps[tt // 2][:, (tt % 2) * D:(tt % 2 + 1) * D], x_sb[:, tt, :],
                                  ALU.add).then_inc(x1_done, 1)
                if tt >= 1:
                    dve.wait_ge(x1_done, tt)
                    dve.bn_stats(stat[:, TT + tt - 1, :], x_sb[:, tt - 1, :]).then_inc(x1_stat, 1)
            dve.wait_ge(x1_done, TT)
            dve.bn_stats(stat[:, 2 * TT - 1, :], x_sb[:, TT - 1, :]).then_inc(x1_stat, 1)
            for tt in range(TT):
                dve.wait_ge(x1_stat, tt + 1)
                dve.bn_aggr(mv[:, TT + tt, :], stat[:, TT + tt, :]).then_inc(x2_mv, 1)
            dve.wait_ge(x2_mv, TT)
            norm_rows(TT, x2_std, x2_n)
            for tt in range(TT):
                dve.wait_ge(y_hi, tt + 1)
                ps = r_ps[tt % 2][:, 0:ND * P].rearrange("p (d q) -> p d q", d=ND)
                dve.tensor_tensor(xnT[:, 1, :, tt * P:(tt + 1) * P], ps, f(xnT[:, 0, :, tt * P:(tt + 1) * P]),
                                  ALU.subtract).then_inc(y_lo, 1)

            def route():
                dve.wait_ge(lg_sc, 1)
                link(dve.tensor_tensor(sfc[:, :, :], sc[:, :, :], bias[:, :].unsqueeze(1).to_broadcast([P, TT, E]), ALU.add))
                for tt in range(TT):
                    for g in range(G):
                        last = dve.max(g8[:, tt, g, :], sfc[:, tt, g * GE:(g + 1) * GE])
                link(last)
                link(dve.tensor_tensor(gs[:, :, 0:G], g8[:, :, :, 0], g8[:, :, :, 1], ALU.add))
                for tt in range(TT):
                    last = dve.max(gtop[:, tt, :], gs[:, tt, :])
                link(last)
                for tt in range(TT):
                    last = dve.max_index(gidx[:, tt, :], gtop[:, tt, :], gs[:, tt, :])
                link(last)
                link(dve.tensor_copy(gidxf[:, :, :], gidx[:, :, :]))
                eq = eq_v[:, 0:TT * G * TOPG].rearrange("p (t g k) -> p t g k", t=TT, k=TOPG)
                link(dve.tensor_tensor(eq, iota[:, 0:G].unsqueeze(1).unsqueeze(3).to_broadcast([P, TT, G, TOPG]),
                                       gidxf[:, :, 0:TOPG].unsqueeze(2).to_broadcast([P, TT, G, TOPG]), ALU.is_equal))
                link(dve.tensor_reduce(gmask[:, :, :], eq, AX.X, ALU.add))
                link(dve.tensor_tensor(masked[:, :, :].rearrange("p t (g e) -> p (t g) e", g=G),
                                       sfc[:, :, :].rearrange("p t (g e) -> p (t g) e", g=G),
                                       gmask[:, :, :].rearrange("p t g -> p (t g)").unsqueeze(2)
                                       .to_broadcast([P, TT * G, GE]), ALU.mult))
                link(dve.tensor_scalar(masked[:, :, :], masked[:, :, :], 0.0, None, ALU.add))
                for tt in range(TT):
                    last = dve.max(etop[:, tt, :], masked[:, tt, :])
                link(last)
                for tt in range(TT):
                    last = dve.max_index(eidx[:, tt, :], etop[:, tt, :], masked[:, tt, :])
                link(last)
                link(dve.tensor_copy(eidxf[:, :, :], eidx[:, :, :]))
                eq = eq_v.rearrange("p (t e k) -> p t e k", t=TT, k=TOPK)
                link(dve.tensor_tensor(eq, iota[:, :].unsqueeze(1).unsqueeze(3).to_broadcast([P, TT, E, TOPK]),
                                       eidxf[:, :, 0:TOPK].unsqueeze(2).to_broadcast([P, TT, E, TOPK]), ALU.is_equal))
                link(dve.tensor_reduce(emask[:, :, :], eq, AX.X, ALU.add))
                link(dve.tensor_tensor(esel[:, :, :], sc[:, :, :], emask[:, :, :], ALU.mult))
                link(dve.tensor_reduce(wsum[:, :, 0], esel[:, :, :], AX.X, ALU.add))
                link(dve.tensor_scalar(wsum[:, :, 1], wsum[:, :, 0], 1e-20, None, ALU.add))
                link(dve.reciprocal(wsum[:, :, 2], wsum[:, :, 1]))
                link(dve.tensor_scalar(wsum[:, :, 2], wsum[:, :, 2], SCALE, None, ALU.mult))
                dve.tensor_tensor(comb[:, :, :], esel[:, :, :], wsum[:, :, 2:3].to_broadcast([P, TT, E]), ALU.mult) \
                   .then_inc(cmb, 1)

            def gate(n):
                dve.wait_ge(h3_mm, n + 1)
                if n >= 1:
                    dve.wait_ge(sw, n)
                else:
                    dve.wait_ge(silu, 1)
                s = rtmp[:, 2 + n % 2, :] if n >= 1 else rtmp[:, 0, :]
                if n >= 2:
                    dve.wait_ge(g_hi, n - 1)
                    dve.wait_ge(g_lo, n - 1)
                dve.tensor_tensor(rtmp[:, 4 + n % 2, :], h_ps[2 * (n % 2) + 1][:, :], s, ALU.mult).then_inc(gated, 1)

            def gate_lo(n):
                dve.wait_ge(g_hi, n + 1)
                dve.tensor_tensor(pT_flat[:, 2 + n % 2, 0:T], rtmp[:, 4 + n % 2, :], f(pT_flat[:, n % 2, 0:T]),
                                  ALU.subtract).then_inc(g_lo, 1)

            dve.wait_ge(d_gate, 48)
            route()
            weight_hi(SPL_M)
            for n in range(NX):
                if SPL_M < n + AHEAD < NX:
                    weight_hi(n + AHEAD)
                gate(n)
                gate_lo(n)
            dve.wait_ge(w2_mm, NX)
            dve.tensor_copy(prob[:, 1, :], acc_ps[1][:, :]).then_inc(fin[1], 1)

        @block.gpsimd
        def _(pool):
            links = [0]

            def link(ins):
                links[0] += 1
                ins.then_inc(chain_p, 1)
                pool.wait_ge(chain_p, links[0])

            pool.wait_ge(d_kv, 32)
            hd = DC // 2
            for b in range(B):
                rows = slice(b * LC, (b + 1) * LC)
                pool.tensor_tensor(kvr[:, rows, 0, :], kv[:, rows, :], kvtab[:, :, 0, :], ALU.mult)
                pool.tensor_tensor(kvr[:, rows, 1, 0:hd], kv[:, rows, hd:DC], kvtab[:, :, 1, 0:hd], ALU.mult)
                link(pool.tensor_tensor(kvr[:, rows, 1, hd:DC], kv[:, rows, 0:hd], kvtab[:, :, 1, hd:DC], ALU.mult))
            link(pool.tensor_tensor(kvr[:, :, 0, :], kvr[:, :, 0, :], kvr[:, :, 1, :], ALU.add))
            pool.tensor_copy(kvr[:, :, 1, :], kvr[:, :, 0, :]).then_inc(kv_roped, 1)

            def ropes(g, c):
                n = NCH * g + c
                pool.wait_ge(wk_out, use(g, "B", c) + 1)
                if g >= 1:
                    pool.wait_ge(wk_full, use(g - 1, "RPP"[c], 3) + 1)
                if g >= ROPE_V:
                    if g == ROPE_V and c == 0:
                        pool.wait_ge(rope_a, NCH * ROPE_V)
                    link(rope_half(pool, link, n, c, 0))
                rope_half(pool, link, n, c, 1).then_inc(rope_p, 1)
                pool.wait_ge(rope_p, n + 1)

            def weight_lo(n):
                if n < SPL_M:
                    pool.wait_ge(d_raw[n], 16)
                    if n == 0:
                        pool.wait_ge(wk_full, Q_DONE[NG - 1])
                    link(pool.tensor_copy(w_slots[n][:, 0, :], raw_v[:, n, :]))
                else:
                    pool.wait_ge(wx_hi, n - SPL_M + 1)
                pool.tensor_tensor(w_slots[n % SPL][:, 1, :], raw_v[:, n % RAW, :], f(w_slots[n % SPL][:, 0, :]),
                                   ALU.subtract).then_inc(wx_lo, 1)

            def weigh(n):
                pool.wait_ge(silu, n + 1)
                e = n - 1
                if e < CB_PE:
                    pool.wait_ge(cb_sb, e + 1)
                else:
                    pool.wait_ge(d_cb[e % CBR], 16 * (e // CBR + (e % CBR >= CB_PE)))
                if n >= 3:
                    pool.wait_ge(gated, n - 1)
                pool.tensor_tensor(rtmp[:, 2 + n % 2, :], rtmp[:, n % 2, :], roped_flat[:, e % CBR, :], ALU.mult) \
                    .then_inc(sw, 1)

            pool.wait_ge(d_rope, 16)
            for g in range(NG):
                for c in range(NCH):
                    ropes(g, c)
            for n in range(SPL_M + 1):
                weight_lo(n)
            for n in range(1, NX):
                weigh(n)
                if n + AHEAD < NX:
                    weight_lo(n + AHEAD)


def rope_tables(length, dim):
    inv = (np.float32(1.0) / np.float32(10000.0) ** (np.arange(0, dim, 2, dtype=np.float32) / np.float32(dim)))
    f = np.arange(length, dtype=np.float32)[:, None] * inv.astype(np.float32)[None, :]
    return np.repeat(np.sin(f), 2, axis=-1), np.repeat(np.cos(f), 2, axis=-1)


def kernel(x, ctx_512, L0_xattn_Wq, L0_xattn_w_kc_q, L0_xattn_w_kc_kv, L0_xattn_W_qr, L0_xattn_W_kr, L0_xattn_Wo,
           L0_ffn_gate_weight, L0_ffn_e_score_correction_bias, L0_ffn_w1, L0_ffn_w3, L0_ffn_w2, L0_ffn_ws1,
           L0_ffn_ws3, L0_ffn_ws2):
    import concourse.bacc as bacc
    from concourse.bass_utils import run_bass_kernel_spmd

    a = np.asarray
    c = np.ascontiguousarray
    f32 = np.float32
    x_l = c(a(x).reshape(TT, P, D).transpose(1, 0, 2))
    kv_l = c(a(ctx_512).reshape(B * LC, P, DC).transpose(1, 0, 2))
    w_attn = np.zeros((NG, P, WGRP), f32)
    wq = a(L0_xattn_Wq).reshape(NG, HG, K, D)
    w_attn[:, :, 0:HG * D] = wq.transpose(0, 2, 1, 3).reshape(NG, K, HG * D)
    w_attn[:, :, HG * D:WM] = a(L0_xattn_w_kc_q).reshape(NG, HG, K, CQ).transpose(0, 2, 1, 3).reshape(NG, K, HG * CQ)
    wqr, wkr = a(L0_xattn_W_qr), a(L0_xattn_W_kr)
    for g in range(NG):
        for m, (ch, j) in enumerate(COMBOS):
            for i in range(2):
                head = 2 * j + i
                lo, hi = max(ch * P, head * HALF), min((ch + 1) * P, (head + 1) * HALF)
                if lo >= hi:
                    continue
                for ab in range(2):
                    col = WM + (m * 2 + ab) * P + lo - ch * P
                    q0 = ab * HALF + lo - head * HALF
                    w_attn[g, i * R:(i + 1) * R, col:col + hi - lo] = wqr[g * HG + head, q0:q0 + hi - lo, :].T
        for j in range(NPG):
            for i in range(2):
                col = WM + NCO * 2 * P + j * P + i * DC
                w_attn[g, i * R:(i + 1) * R, col:col + DC] = wkr[g * HG + 2 * j + i].T
    o = WM + WG
    w_attn[:, :, o:o + HG * DC] = a(L0_xattn_w_kc_kv).reshape(NG, HG, K, DC).transpose(0, 2, 1, 3).reshape(NG, K, HG * DC)
    w_attn[:, :, o + HG * DC:] = a(L0_xattn_Wo).T.reshape(NG, HG, K, D).transpose(0, 2, 1, 3).reshape(NG, K, HG * D)
    gate_l = c(a(L0_ffn_gate_weight).T.reshape(ND, P, E).transpose(1, 0, 2))
    bias_l = c(np.broadcast_to(a(L0_ffn_e_score_correction_bias), (P, E)))
    w1 = np.concatenate([a(L0_ffn_ws1)[None], a(L0_ffn_w1)])
    w3 = np.concatenate([a(L0_ffn_ws3)[None], a(L0_ffn_w3)])
    w2 = np.concatenate([a(L0_ffn_ws2)[None], a(L0_ffn_w2)])
    w_exp = np.concatenate([w.transpose(0, 2, 1).reshape(NX, ND, P, I).transpose(0, 2, 1, 3).reshape(NX, P, ND * I)
                            for w in (w1, w3)] + [w2.transpose(0, 2, 1)], axis=2)

    sin_q, cos_q = rope_tables(S, CQ)
    rope_q = np.zeros((P, NCH, 4, S), f32)
    for ch in range(NCH):
        i = (ch * P + np.arange(P)) % HALF
        rope_q[:, ch, 0], rope_q[:, ch, 1] = cos_q.T[i], -sin_q.T[i]
        rope_q[:, ch, 2], rope_q[:, ch, 3] = cos_q.T[i + HALF], sin_q.T[i + HALF]
    sin_k, cos_k = rope_tables(L, DC)
    sign = np.where(np.arange(DC) < DC // 2, f32(-1), f32(1))
    rope_kv = c(np.stack([cos_k, sin_k * sign], 1).reshape(LC, P, 2, DC).transpose(1, 0, 2, 3).astype(f32))
    ident = np.eye(P, dtype=f32)
    iota = c(np.broadcast_to(np.arange(E, dtype=f32), (P, E)))

    nc = bacc.Bacc("TRN2", target_bir_lowering=False, num_devices=1)
    arrays = {"x": x_l, "ctx_kv": kv_l, "w_attn": w_attn, "w_gate": gate_l, "gate_bias": bias_l, "w_exp": c(w_exp),
              "rope_q": rope_q, "rope_kv": rope_kv, "ident": ident, "iota": iota}
    aps = [nc.dram_tensor(f"in_{n}", v.shape, mybir.dt.from_np(v.dtype), kind="ExternalInput").ap()
           for n, v in arrays.items()]
    c_dram = nc.dram_tensor("combine_scratch", (E, T), F32, kind="Internal").ap()
    out = nc.dram_tensor("out_T", (D, T), F32, kind="ExternalOutput").ap()
    build(nc, *aps, c_dram, out)
    r = run_bass_kernel_spmd(nc, [{f"in_{n}": v for n, v in arrays.items()}], core_ids=[0])
    return r.results[0]["out_T"].T.reshape(B, S, D)
```

```python
from contextlib import ExitStack

import numpy as np
import concourse.bass as bass
from concourse import mybir

ALU = mybir.AluOpType
ACT = mybir.ActivationFunctionType
AX = mybir.AxisListType
F32 = mybir.dt.float32
F32R = mybir.dt.float32r
U32 = mybir.dt.uint32

P = 128
B, S, D = 2, 256, 256
L, DC = 512, 64
H, K, R, CQ = 16, 128, 64, 192
T = B * S
TT = T // P
ND = D // P
LC = L // P
HALF = CQ // 2
E, G, GE, TOPG, TOPK, I = 32, 4, 8, 2, 4, 128
SCALE = 2.5
EPS = 1e-5

HG = 4
NG = H // HG
NPG = HG // 2
NP = H // 2
NQT = 3
TAIL = 2 * HALF - P
WM = HG * (D + CQ)
WG = NPG * NQT * P + NPG * P
WN = HG * (DC + D)
WGRP = WM + WG + WN
ORDER_0 = ("M0", "M1", "A0", "B0", "C0", "G0", "M2", "M3", "R2", "A1", "B1", "C1", "G1", "P2", "N0", "N1")
ORDER = ("M0", "M1", "A0", "B0", "G0", "C0", "M2", "M3", "A1", "B1", "R2", "C1", "G1", "P2", "N0", "N1")
USES = len(ORDER)
TILES = H * B * (S // P)
TPG = TILES // NG
WE = 2 * ND * I + D
NX = E + 1
RAW = 6
SPL_M, SPL = 3, 6
POOL_HI = 5
AHEAD = 3
ROPE_V = 1
LOOK = 3
CB_PE = 2
CBR = 6
PERIOD = 6
LOOP_1, LOOP_N = 5, 4
LOOP_E = LOOP_1 + LOOP_N * PERIOD


def build(nc, x, ctx_kv, w_attn, w_gate, gate_bias, w_exp, rope_q, rope_kv, ident_in, iota_in, c_dram, out):
    with ExitStack() as stack:
        def sb(name, shape, dt=F32):
            return stack.enter_context(nc.sbuf_tensor(name, shape, dt))

        def sem(name):
            return stack.enter_context(nc.semaphore(name))

        x_sb = sb("x_sb", [P, TT, D])
        xn = sb("xn", [P, TT, D])
        xnT = sb("xnT", [P, 2, ND, T], F32R)
        wring = sb("wring", [P, 2 * WGRP])
        msplit = sb("msplit", [P, SPL_M * 2 * WE], F32R)
        gmat = sb("gmat", [P, NPG, NQT, P])
        nmat = sb("nmat", [P, NP, D])
        rope = sb("rope", [P, NQT, 2, S])
        abuf = sb("abuf", [P, 2, NQT + 1, T])
        rtmp = sb("rtmp", [P, 6, T])
        roped = sb("roped", [P, NPG, NQT, T])
        qsp = sb("qsp", [P, 4, 2, T], F32R)
        kdup = sb("kdup", [P, 2, B * L], F32R)
        kvs = sb("kvs", [P, B * LC, P], F32R)
        prob = sb("prob", [P, 3, L])
        pT = sb("pT", [P, 2, 2, LC, S], F32R)
        ctmp = sb("ctmp", [P, 2, S])
        ctT = sb("ctT", [P, NP, T])
        kv = sb("kv", [P, B * LC, DC])
        kvr = sb("kvr", [P, B * LC, 2, DC])
        kvtab = sb("kvtab", [P, LC, 2, DC])
        ident = sb("ident", [P, P])
        iota = sb("iota", [P, E])
        gateT = sb("gateT", [P, ND, E])
        bias = sb("bias", [P, E])
        stat = sb("stat", [P, 2 * TT, 6])
        mv = sb("mv", [P, 2 * TT, 2])
        std = sb("std", [P, 2 * TT, 1])
        rstd = sb("rstd", [P, 2 * TT, 1])
        nmax = sb("nmax", [P, TILES])
        psum_e = sb("psum_e", [P, TILES])
        rsum = sb("rsum", [P, TILES])
        sc = sb("sc", [P, TT, E])
        sfc = sb("sfc", [P, TT, E])
        g8 = sb("g8", [P, TT, G, 8])
        gs = sb("gs", [P, TT, 8])
        gtop = sb("gtop", [P, TT, 8])
        gidx = sb("gidx", [P, TT, 8], U32)
        gidxf = sb("gidxf", [P, TT, 8])
        gmask = sb("gmask", [P, TT, G])
        masked = sb("masked", [P, TT, E])
        etop = sb("etop", [P, TT, 8])
        eidx = sb("eidx", [P, TT, 8], U32)
        eidxf = sb("eidxf", [P, TT, 8])
        emask = sb("emask", [P, TT, E])
        esel = sb("esel", [P, TT, E])
        wsum = sb("wsum", [P, TT, 3])
        comb = sb("comb", [P, TT, E])
        combT = prob[0:E, 2, :]
        epsc = sb("epsc", [P, 1])
        warm = sb("warm", [P, 2])

        bank = [stack.enter_context(nc.psum_tensor(f"bank{i}", [P, 512], F32)) for i in range(8)]
        work = bank[0:2]
        s_ps = bank[2:5]
        t_ps = bank[5:7]
        pv_ps = bank[7]
        h_ps = bank[0:4]
        r_ps = bank[3:5]
        cb_ps = (bank[4], bank[7])
        o_ps = bank[0:2]
        acc_ps = bank[5:7]
        g_ps = bank[7]

        def half_of(g):
            return (g % 2) * WGRP

        def wq(g, i, dc):
            a = half_of(g) + i * (D + CQ) + dc * P
            return wring[:, a:a + P]

        def wkcq(g, i):
            a = half_of(g) + i * (D + CQ) + D
            return wring[:, a:a + CQ]

        def wqrT(g, j, k):
            a = half_of(g) + WM + (j * NQT + k) * P
            return wring[:, a:a + P]

        def wkrT(g, j):
            a = half_of(g) + WM + NPG * NQT * P + j * P
            return wring[:, a:a + P]

        def wkv(g, i):
            a = half_of(g) + WM + WG + i * DC
            return wring[:, a:a + DC]

        def woT(g, i):
            a = half_of(g) + WM + WG + HG * DC + i * D
            return wring[:, a:a + D]

        qsp_flat = qsp[:, :, :, :].rearrange("p a b t -> p (a b t)")
        m_v = msplit[:, 0:2 * ND * NPG * NQT * P].rearrange("p (s d j k n) -> p s d j k n", s=2, d=ND, j=NPG, k=NQT)
        w_slots = [t.rearrange("p (s n) -> p s n", s=2) for t in
                   [msplit[:, r * 2 * WE:(r + 1) * 2 * WE] for r in range(SPL_M)] +
                   [qsp_flat[:, r * 2 * WE:(r + 1) * 2 * WE] for r in range(SPL - SPL_M - 1)] +
                   [kdup[:, :, :].rearrange("p a t -> p (a t)")[:, 0:2 * WE]]]
        raw_v = wring[:, 0:RAW * WE].rearrange("p (r n) -> p r n", r=RAW)
        roped_flat = roped[:, :, :, :].rearrange("p j k t -> p (j k) t")
        pT_flat = pT[:, :, :, :, :].rearrange("p s b c q -> p (s b) (c q)")
        eq_v = prob[:, 0, :]

        probs = [prob[:, 0, :], prob[:, 1, :], prob[:, 2, :], xn[:, 0:2, :].rearrange("p t d -> p (t d)")]
        xT_f = abuf[:, 0, 0:ND, :]
        xn_out = [prob[:, 0, :], prob[:, 1, :]]

        def pv_of(hb):
            bk = s_ps[1 + hb % 2] if hb >= TILES // 2 - 2 else pv_ps
            return bk[:, (hb % 2) * S:(hb % 2 + 1) * S]

        def f(ap):
            return ap.bitcast(F32)

        d_x = sem("d_x"); d_kv = sem("d_kv"); d_const = sem("d_const"); d_rope = sem("d_rope"); d_gate = sem("d_gate")
        d_wm = [[sem(f"d_wm{i}_{j}") for j in range(HG)] for i in range(2)]
        d_wg = [sem(f"d_wg{i}") for i in range(2)]
        d_wn = [sem(f"d_wn{i}") for i in range(2)]
        d_raw = [sem(f"d_raw{i}") for i in range(RAW)]
        d_ct = sem("d_ct"); d_cb = [sem(f"d_cb{i}") for i in range(CBR)]
        d_out = sem("d_out")
        chain_v = sem("chain_v")
        chain_p = sem("chain_p")
        ln_std = sem("ln_std"); ln_mv = sem("ln_mv"); ln_xn = sem("ln_xn")
        kv_roped = sem("kv_roped"); kv_split = sem("kv_split")
        xT_mm = sem("xT_mm"); xT_hi = sem("xT_hi"); xT_lo = sem("xT_lo")
        kT_mm = sem("kT_mm"); kT_hi = sem("kT_hi"); kT_lo = sem("kT_lo")
        wk_full = sem("wk_full"); wk_out = sem("wk_out"); m_lo = sem("m_lo")
        rope_a = sem("rope_a"); rope_p = sem("rope_p")
        q_lo = sem("q_lo")
        s_mm = sem("s_mm"); s_max = sem("s_max"); s_exp = sem("s_exp"); s_inv = sem("s_inv"); s_norm = sem("s_norm")
        t_mm = sem("t_mm"); t_hi = sem("t_hi"); t_lo = sem("t_lo")
        pv_mm = sem("pv_mm"); c_half = sem("c_half"); c_sum = sem("c_sum")
        o_mm = sem("o_mm"); x1_done = sem("x1_done"); x1_stat = sem("x1_stat"); x2_std = sem("x2_std"); x2_mv = sem("x2_mv"); x2_n = sem("x2_n")
        y_mm = sem("y_mm"); y_fa = sem("y_fa"); y_fv = sem("y_fv"); y_hi = sem("y_hi"); y_lo = sem("y_lo")
        lg_mm = sem("lg_mm"); lg_sc = sem("lg_sc"); cmb = sem("cmb"); ct_mm = sem("ct_mm"); ct_sb = sem("ct_sb")
        cb_mm = sem("cb_mm"); wx_hi = sem("wx_hi"); wx_lo = sem("wx_lo")
        h1_mm = sem("h1_mm"); h3_mm = sem("h3_mm"); silu = sem("silu"); sw = sem("sw"); weighed = sem("weighed"); gated = sem("gated")
        g_hi = sem("g_hi"); g_lo = sem("g_lo"); w2_mm = sem("w2_mm"); fin = [sem(f"fin{i}") for i in range(ND)]

        PLAN = [
            {1: "-C1 -G1", 2: "-P0", 3: "-P1 -P2", 4: "-N0 -N1 M0 M1", 5: "A0 B0 G0", 6: "C0", 7: "M2 M3", 8: "A1",
             9: "B1", 10: "R0 R1", 11: "R2 C1", 12: "G1", 13: "P0", 14: "P1", 15: "P2"},
            {0: "-N0", 1: "-N1", 2: "M0 M1", 4: "A0 B0", 6: "G0 C0 M2", 7: "M3", 9: "A1 B1", 10: "R0 R1",
             11: "R2 C1", 12: "G1", 14: "P0", 15: "P1 P2"},
            {0: "-N0", 1: "-N1", 2: "M0 M1", 4: "A0 B0", 6: "G0 C0 M2", 7: "M3", 9: "A1 B1", 10: "R0 R1",
             11: "R2 C1", 12: "G1", 14: "P0", 15: "P1 P2"},
            {0: "-N0", 1: "-N1", 3: "O0 O1", 5: "O2 O3", 8: "O4", 10: "O5", 12: "O6"},
        ]

        def steps(t):
            g = t // TPG
            for s in PLAN[g].get(t % TPG, "").split():
                yield (g, s[1], int(s[2])) if s[0] == "-" else (g + 1, s[0], int(s[1]))

        PROLOGUE = [(0, s[0], int(s[1])) for s in "M0 X0 M1 A0 B0 C0 G0 M2 K0 M3 R0 R1 R2 A1 V0 B1".split()]

        def use(g, kind, i):
            return USES * g + (ORDER if g else ORDER_0).index(f"{kind}{i}")

        N_DONE = [use(g, "N", 1) + 1 for g in range(NG)]
        Q_DONE = [use(g, "C", 1) + 1 for g in range(NG)]

        def m_parts(u, i):
            src = work[u % 2][:, 0:ND * CQ].rearrange("p (d a n) -> p d a n", d=ND, a=2)
            j = i // 2
            if i % 2 == 0:
                return [(m_v[:, 0, :, j, 0:2, 0:HALF], m_v[:, 1, :, j, 0:2, 0:HALF], src)]
            n = HALF - TAIL
            hi, lo = (m_v[:, s, :, j, 2, :].rearrange("p d (a n) -> p d a n", a=2) for s in range(2))
            return [(m_v[:, 0, :, j, 0:2, HALF:P], m_v[:, 1, :, j, 0:2, HALF:P], src[:, :, :, 0:n]),
                    (hi, lo, src[:, :, :, n:HALF])]

        def over_experts(eng, first, body):
            for n in range(first, LOOP_1):
                body(n, n % PERIOD, n // PERIOD)
            with eng.Fori(0, LOOP_N) as k:
                for n in range(LOOP_1, LOOP_1 + PERIOD):
                    body(n + PERIOD * k, n % PERIOD, n // PERIOD + k)
            for n in range(LOOP_E, NX):
                body(n, n % PERIOD, n // PERIOD)

        def peeled(n):
            return isinstance(n, int)

        block = stack.enter_context(nc.Block())

        def rope_tile(eng, link, g, j, k, scratch):
            if g >= 1:
                eng.wait_ge(wk_full, use(g - 1, "RP"[j], 2) + 1)
            own, other = abuf[:, j, k, :], abuf[:, j, (1, 0, 3)[k], :]
            cos = rope[:, k, 0, :].unsqueeze(1).to_broadcast([P, B, S])
            sin = rope[:, k, 1, :].unsqueeze(1).to_broadcast([P, B, S])
            t0, t1 = rtmp[:, scratch, :], rtmp[:, scratch + 1, :]
            eng.tensor_tensor(t0.rearrange("p (b s) -> p b s", b=B), own.rearrange("p (b s) -> p b s", b=B), cos, ALU.mult)
            link(eng.tensor_tensor(t1.rearrange("p (b s) -> p b s", b=B), other.rearrange("p (b s) -> p b s", b=B), sin,
                                   ALU.mult))
            return eng.tensor_tensor(roped[:, j, k, :], t0, t1, ALU.add)

        def await_roped(eng, p, k):
            if p >= ROPE_V:
                eng.wait_ge(rope_p, ROPE_V + NQT * (p - ROPE_V) + k + 1)
            elif k == 1:
                eng.wait_ge(rope_p, p + 1)
            else:
                eng.wait_ge(rope_a, 2 * p + k // 2 + 1)

        @block.sync
        def _(sp):
            sp.dma_start(x_sb[:, :, :], x).then_inc(d_x, 16)

            def load_group(g, part):
                if part[0] == "m":
                    a, n, s = int(part[1]) * (D + CQ), D + CQ, d_wm[g % 2][int(part[1])]
                else:
                    a, n, s = {"g": (WM, WG, d_wg[g % 2]), "n": (WM + WG, WN, d_wn[g % 2])}[part]
                sp.dma_start(wring[:, half_of(g) + a:half_of(g) + a + n], w_attn[g, :, a:a + n]).then_inc(s, 16)

            load_group(0, "m0")
            sp.dma_start(ident[:, :], ident_in).then_inc(d_const, 16)
            for i in range(1, HG):
                load_group(0, f"m{i}")
            sp.dma_start(kv[:, :, :], ctx_kv).then_inc(d_kv, 16)
            sp.dma_start(kvtab[:, :, :, :], rope_kv).then_inc(d_kv, 16)
            sp.dma_start(rope[:, :, :, :], rope_q).then_inc(d_rope, 16)
            load_group(0, "g")
            load_group(0, "n")
            for part in ("m0", "m1", "m2", "m3", "g", "n"):
                load_group(1, part)
            sp.dma_start(gateT[:, :, :], w_gate).then_inc(d_gate, 16)
            sp.dma_start(bias[:, :], gate_bias).then_inc(d_gate, 16)
            sp.dma_start(iota[:, :], iota_in).then_inc(d_gate, 16)
            for g in range(2, NG):
                sp.wait_ge(wk_full, N_DONE[g - 2])
                for part in ("m0", "m1", "m2", "m3", "g", "n"):
                    load_group(g, part)

            def load_w(n, r):
                sp.wait_ge(wx_lo, n - RAW + 1)
                sp.dma_start(raw_v[:, r, :], w_exp[n]).then_inc(d_raw[r], 16)

            def load_cb(e, r):
                if not (peeled(e) and e - CBR < CB_PE):
                    sp.wait_ge(sw, e - CBR - CB_PE + 1)
                sp.dma_start(roped_flat[:, r, :], c_dram[e].unsqueeze(0).to_broadcast([P, T])).then_inc(d_cb[r], 16)

            for n in range(RAW):
                last = NG - 2 if (n + 1) * WE <= WGRP else NG - 1
                sp.wait_ge(wk_full, N_DONE[last])
                sp.dma_start(raw_v[:, n, :], w_exp[n]).then_inc(d_raw[n], 16)
            sp.wait_ge(ct_sb, 1)
            sp.dma_start(c_dram, combT).then_inc(d_ct, 16)
            sp.wait_ge(d_ct, 16)
            for e in range(CB_PE, CBR):
                sp.dma_start(roped_flat[:, e, :], c_dram[e:e + 1, :].to_broadcast([P, T])).then_inc(d_cb[e], 16)
            for n in range(RAW, RAW + CB_PE):
                load_w(n, n % RAW)
                load_cb(n, n % CBR)
            with sp.Fori(0, LOOP_N) as k:
                for n in range(RAW + CB_PE, RAW + CB_PE + PERIOD):
                    load_w(n + PERIOD * k, n % RAW)
                    load_cb(n + PERIOD * k, n % CBR)
            for n in range(RAW + CB_PE + LOOP_N * PERIOD, NX):
                load_w(n, n % RAW)
            for dc in range(ND):
                sp.wait_ge(fin[dc], 1)
                sp.dma_start(out[dc * P:(dc + 1) * P, :], xn_out[dc]).then_inc(d_out, 16)
            sp.wait_ge(d_out, 16 * ND)

        @block.tensor
        def _(pe):
            def split3(out_ap, a_hi, a_lo, b_hi, b_lo, first, last):
                pe.matmul(out_ap, a_hi, b_hi, start=first, stop=False)
                pe.matmul(out_ap, a_hi, b_lo, start=False, stop=False)
                return pe.matmul(out_ap, a_lo, b_hi, start=False, stop=last)

            def bank_free(u):
                if u >= 2:
                    g, k = divmod(u - 2, USES)
                    kind, i = (ORDER if g else ORDER_0)[k]
                    if kind == "M":
                        pe.wait_ge(m_lo, HG * g + int(i) + 1)
                    elif kind in "RP":
                        pe.wait_ge(q_lo, NPG * g + "RP".index(kind) + 1)
                    else:
                        pe.wait_ge(wk_out, u - 1)

            def step(g, kind, i):
                if kind in "MGABCN":
                    u = use(g, kind, i)
                    bank_free(u)
                if kind == "M":
                    pe.wait_ge(d_wm[g % 2][i], 16 * (g // 2 + 1))
                    for dc in range(ND):
                        mm = pe.matmul(work[u % 2][:, dc * CQ:(dc + 1) * CQ], wq(g, i, dc), wkcq(g, i),
                                       start=True, stop=True)
                    mm.then_inc(wk_full, 1)
                elif kind == "G":
                    pe.wait_ge(d_wg[g % 2], 16 * (g // 2 + 1))
                    for k in range(NQT):
                        mm = pe.matmul(work[u % 2][:, k * P:(k + 1) * P], wqrT(g, i, k), wkrT(g, i), start=True, stop=True)
                    mm.then_inc(wk_full, 1)
                elif kind == "N":
                    pe.wait_ge(d_wn[g % 2], 16 * (g // 2 + 1))
                    for k in range(2):
                        mm = pe.matmul(work[u % 2][k * DC:(k + 1) * DC, 0:D], wkv(g, 2 * i + k), woT(g, 2 * i + k),
                                       start=True, stop=True)
                    mm.then_inc(wk_full, 1)
                elif kind in "ABC":
                    k = "ABC".index(kind)
                    pe.wait_ge(m_lo, HG * g + 2 * i + 2)
                    if g == 0:
                        pe.wait_ge(xT_lo, ND)
                    for dc in range(ND):
                        mm = split3(work[u % 2][:, :], m_v[:, 0, dc, i, k, :], m_v[:, 1, dc, i, k, :],
                                    xnT[:, 0, dc, :], xnT[:, 1, dc, :], dc == 0, dc == ND - 1)
                    mm.then_inc(wk_full, 1)
                elif kind in "RP":
                    j = "RP".index(kind)
                    u = use(g, kind, 2)
                    if i == 0:
                        bank_free(u)
                        pe.wait_ge(wk_out, use(g, "G", j) + 1)
                    await_roped(pe, NPG * g + j, i)
                    mm = pe.matmul(work[u % 2][:, :], gmat[:, j, i, :], roped[:, j, i, :],
                                   start=(i == 0), stop=(i == NQT - 1))
                    if i == NQT - 1:
                        mm.then_inc(wk_full, 1)
                elif kind == "X":
                    pe.wait_ge(d_const, 16)
                    for tt in range(TT):
                        pe.wait_ge(ln_xn, tt + 1)
                        for dc in range(ND):
                            mm = pe.transpose(t_ps[dc][:, tt * P:(tt + 1) * P], xn[:, tt, dc * P:(dc + 1) * P], ident[:, :])
                    mm.then_inc(xT_mm, 1)
                elif kind == "K":
                    pe.wait_ge(kv_roped, 1)
                    for n in range(B * LC):
                        mm = pe.transpose(s_ps[n // LC][:, (n % LC) * P:(n % LC + 1) * P],
                                          kvr[:, n, :, :].rearrange("p a c -> p (a c)"), ident[:, :])
                    mm.then_inc(kT_mm, 1)
                elif kind == "O":
                    pe.wait_ge(wk_out, USES * NG)
                    pe.wait_ge(q_lo, NP)
                    pe.wait_ge(c_sum, 4 * i + 4)
                    for tt in range(TT):
                        mm = pe.matmul(o_ps[tt // 2][:, (tt % 2) * D:(tt % 2 + 1) * D], ctT[:, i, tt * P:(tt + 1) * P],
                                       nmat[:, i, :], start=(i == 0 and tt % 2 == 0), stop=(i == NP - 1 and tt % 2 == 1),
                                       skip_group_check=True)
                        if i == NP - 1 and tt % 2 == 1:
                            mm.then_inc(o_mm, 1)

            def scores(t):
                h, b, st = t // 4, (t // 2) % 2, t % 2
                pe.wait_ge(q_lo, h // 2 + 1)
                if t == 0:
                    pe.wait_ge(kT_lo, 2)
                if t >= 3:
                    pe.wait_ge(s_exp, t - 2)
                q = qsp[:, (h // 2) % 4, h % 2, b * S + st * P:b * S + (st + 1) * P]
                pe.matmul(s_ps[t % 3][:, :], q, kdup[:, 0, b * L:(b + 1) * L], start=True, stop=False)
                pe.matmul(s_ps[t % 3][:, :], q, kdup[:, 1, b * L:(b + 1) * L], start=False, stop=True) \
                  .then_inc(s_mm, 1)

            def transposes(t):
                pe.wait_ge(s_norm, t + 1)
                if t >= 2:
                    pe.wait_ge(t_lo, t - 1)
                for lc in range(LC):
                    mm = pe.transpose(t_ps[t % 2][:, lc * P:(lc + 1) * P], probs[t % 4][:, lc * P:(lc + 1) * P],
                                      ident[:, :])
                mm.then_inc(t_mm, 1)

            def attend(hb):
                b = hb % 2
                pe.wait_ge(t_lo, 2 * hb + 2)
                if hb == 0:
                    pe.wait_ge(kv_split, 2)
                if hb >= TILES // 2 - 2:
                    pe.wait_ge(s_exp, TILES - 1)
                elif hb >= 1:
                    pe.wait_ge(c_sum, hb)
                for n in range(2 * LC):
                    lc, hl = n // 2, n % 2
                    mm = pe.matmul(pv_of(hb), kvs[:, b * LC + lc, :], pT[:, hl, hb % 2, lc, :],
                                   start=(n == 0), stop=(n == 2 * LC - 1))
                mm.then_inc(pv_mm, 1)

            for s in PROLOGUE:
                step(*s)
            pe.wait_ge(kT_lo, 2)
            for t in range(LOOK):
                scores(t)
            for t in range(TILES):
                if t + LOOK < TILES:
                    scores(t + LOOK)
                for s in steps(t):
                    step(*s)
                transposes(t)
                if t % 2 == 1 and t >= 3:
                    attend((t - 3) // 2)
            attend(TILES // 2 - 1)

            step(NG, "O", NP - 1)

            def rows_T(k):
                pe.wait_ge(x2_n, 2 * k + 2)
                for tt in range(2 * k, 2 * k + 2):
                    for dc in range(ND):
                        mm = pe.transpose(r_ps[k][:, (dc * 2 + tt % 2) * P:(dc * 2 + tt % 2 + 1) * P],
                                          xn[:, tt, dc * P:(dc + 1) * P], ident[:, :])
                mm.then_inc(y_mm, 1)

            def seed(tt):
                pe.wait_ge(x1_done, tt + 1)
                for dc in range(ND):
                    pe.matmul(acc_ps[dc][:, tt * P:(tt + 1) * P], x_sb[:, tt, dc * P:(dc + 1) * P], ident[:, :],
                              start=(tt == 0), stop=False, skip_group_check=True)

            def logits(tt):
                for dc in range(ND):
                    mm = pe.matmul(g_ps[:, tt * E:(tt + 1) * E], xT_f[:, dc, tt * P:(tt + 1) * P], gateT[:, dc, :],
                                   start=(dc == 0), stop=(dc == ND - 1))
                mm.then_inc(lg_mm, 1)

            def expert_in(n, r):
                if not (peeled(n) and n < 2):
                    pe.wait_ge(gated, n - 1)
                pe.wait_ge(wx_lo, n + 1)
                for w, signal in ((0, h1_mm), (1, h3_mm)):
                    for dc in range(ND):
                        a = (w * ND + dc) * I
                        mm = split3(h_ps[2 * (r % 2) + w][:, :], w_slots[r][:, 0, a:a + I], w_slots[r][:, 1, a:a + I],
                                    xnT[:, 0, dc, :], xnT[:, 1, dc, :], dc == 0, dc == ND - 1)
                    mm.then_inc(signal, 1)

            def expert_out(n, r):
                last = peeled(n) and n == NX - 1
                pe.wait_ge(g_lo, n + 1)
                for dc in range(ND):
                    a = 2 * ND * I + dc * P
                    w_hi, w_lo = w_slots[r][:, 0, a:a + P], w_slots[r][:, 1, a:a + P]
                    gh, gl = pT_flat[:, r % 2, 0:T], pT_flat[:, 2 + r % 2, 0:T]
                    for k, (wp, gp) in enumerate(((w_hi, gh), (w_hi, gl), (w_lo, gh))):
                        mm = pe.matmul(acc_ps[dc][:, :], wp, gp, start=False, stop=(last and k == 2),
                                       skip_group_check=True)
                    if last or dc == ND - 1:
                        mm.then_inc(w2_mm, 1)

            def in_and_out(n, r, _):
                if not (peeled(n) and n + 2 >= NX):
                    expert_in(n + 2, (r + 2) % PERIOD)
                expert_out(n, r)

            for tt in range(TT):
                seed(tt)
            for k in range(TT // 2):
                rows_T(k)
            pe.wait_ge(d_gate, 48)
            for k, landed in enumerate((y_fa, y_fv)):
                pe.wait_ge(landed, 1)
                for tt in range(2 * k, 2 * k + 2):
                    logits(tt)
            pe.wait_ge(y_lo, TT // 2)
            for n in range(3):
                expert_in(n, n)
            pe.wait_ge(cmb, 1)
            pe.wait_ge(lg_sc, 1)
            for tt in range(TT):
                mm = pe.transpose(g_ps[0:E, tt * P:(tt + 1) * P], comb[:, tt, :], ident[:, :])
            mm.then_inc(ct_mm, 1)
            expert_out(0, 0)
            pe.wait_ge(ct_sb, 1)
            for e in range(CB_PE):
                pe.matmul(cb_ps[e][:, :], ident[0:E, e:e + 1].to_broadcast([E, P]), combT, start=True, stop=True) \
                  .then_inc(cb_mm, 1)
            over_experts(pe, 1, in_and_out)

        @block.scalar
        def _(act):
            act.wait_ge(ln_mv, TT)
            act.activation(std[:, 0:TT, 0], mv[:, 0:TT, 1], ACT.Sqrt, bias=epsc[:, :]).then_inc(ln_std, 1)
            act.activation(warm[:, 0:1], epsc[:, :], ACT.Exp)

            def step(g, kind, i):
                if kind in "MGABCN":
                    u = use(g, kind, i)
                    act.wait_ge(wk_full, u + 1)
                if kind == "M":
                    if g >= 1:
                        act.wait_ge(wk_full, Q_DONE[g - 1])
                    parts = m_parts(u, i)
                    for dst, _, src in parts[:-1]:
                        act.copy(dst, src)
                    act.copy(parts[-1][0], parts[-1][2]).then_inc(wk_out, 1)
                elif kind == "G":
                    if g >= 1:
                        act.wait_ge(wk_full, use(g - 1, "RP"[i], 2) + 1)
                    act.copy(gmat[:, i, :, :].rearrange("p k n -> p (k n)"), work[u % 2][:, 0:NQT * P]).then_inc(wk_out, 1)
                elif kind == "N":
                    act.copy(nmat[:, NPG * g + i, :], work[u % 2][:, 0:D]).then_inc(wk_out, 1)
                elif kind in "AB":
                    if g >= 1:
                        await_roped(act, NPG * (g - 1) + i, 0)
                        await_roped(act, NPG * (g - 1) + i, 1)
                    act.copy(abuf[:, i, "AB".index(kind), :], work[u % 2][:, :]).then_inc(wk_out, 1)
                elif kind == "C":
                    if g >= 1:
                        await_roped(act, NPG * (g - 1) + i, 2)
                    act.copy(abuf[:, i, 2, :], work[u % 2][:, :])
                    act.copy(abuf[0:TAIL, i, 3, :], work[u % 2][TAIL:P, :])
                    act.copy(abuf[TAIL:P, i, 3, :], work[u % 2][0:TAIL, :]).then_inc(wk_out, 1)
                elif kind in "RP" and i == NQT - 1:
                    p = NPG * g + "RP".index(kind)
                    u = use(g, kind, i)
                    act.wait_ge(wk_full, u + 1)
                    if p >= 4:
                        act.wait_ge(s_mm, 8 * (p - 3))
                    act.copy(qsp[0:R, p % 4, 0, :], work[u % 2][0:R, :])
                    act.copy(qsp[R:P, p % 4, 1, :], work[u % 2][R:P, :]).then_inc(wk_out, 1)

                elif kind == "X":
                    act.wait_ge(xT_mm, 1)
                    for dc in range(ND):
                        act.copy(xnT[:, 0, dc, :], t_ps[dc][:, :]).then_inc(xT_hi, 1)
                elif kind == "K":
                    act.wait_ge(kT_mm, 1)
                    for n in range(2):
                        act.copy(kdup[:, 0, n * L:(n + 1) * L], s_ps[n][:, :]).then_inc(kT_hi, 1)

            def exps(t):
                act.wait_ge(s_max, t + 1)
                if t >= 4:
                    act.wait_ge(t_mm, t - 3)
                act.activation(probs[t % 4], s_ps[t % 3][:, :], ACT.Exp, bias=nmax[:, t:t + 1],
                               accum_out=psum_e[:, t:t + 1]).then_inc(s_exp, 1)

            def prob_hi(t):
                hb = t // 2
                act.wait_ge(t_mm, t + 1)
                if hb >= 2:
                    act.wait_ge(pv_mm, hb - 1)
                act.copy(pT[:, 0, hb % 2, :, (t % 2) * P:(t % 2 + 1) * P],
                         t_ps[t % 2][:, :].rearrange("p (c q) -> p c q", c=LC)).then_inc(t_hi, 1)

            def ctx_half(hb):
                h, b = divmod(hb, 2)
                act.wait_ge(pv_mm, hb + 1)
                if hb >= 2:
                    act.wait_ge(c_sum, hb - 1)
                dst, src = (0, DC) if h % 2 == 0 else (DC, 0)
                act.copy(ctmp[dst:dst + DC, hb % 2, :], pv_of(hb)[src:src + DC, :]).then_inc(c_half, 1)

            for s in PROLOGUE:
                step(*s)
            for t in range(LOOK):
                exps(t)
            for t in range(TILES):
                if t + LOOK < TILES:
                    exps(t + LOOK)
                if t % 2 == 0 and t >= 4:
                    ctx_half((t - 4) // 2)
                for s in steps(t):
                    step(*s)
                prob_hi(t)
            ctx_half(TILES // 2 - 2)
            ctx_half(TILES // 2 - 1)

            act.wait_ge(x2_mv, TT)
            act.activation(std[:, TT:2 * TT, 0], mv[:, TT:2 * TT, 1], ACT.Sqrt, bias=epsc[:, :]).then_inc(x2_std, 1)
            act.activation(warm[:, 1:2], epsc[:, :], ACT.Sigmoid)
            for k in range(TT // 2):
                ps = r_ps[k][:, :].rearrange("p (d q) -> p d q", d=ND)
                cols = slice(2 * k * P, (2 * k + 2) * P)
                act.wait_ge(y_mm, k + 1)
                if k == 0:
                    act.copy(xT_f[:, :, cols], ps).then_inc(y_fa, 1)
                else:
                    act.wait_ge(y_fv, 1)
                act.copy(xnT[:, 0, :, cols], ps).then_inc(y_hi, 1)
            act.wait_ge(lg_mm, TT)
            act.activation(sc[:, :, :].rearrange("p t e -> p (t e)"), g_ps[:, 0:TT * E], ACT.Sigmoid).then_inc(lg_sc, 1)

            def silus(n, r):
                act.wait_ge(h1_mm, n + 1)
                if not (peeled(n) and n < 2):
                    act.wait_ge(gated, n - 1)
                act.activation(rtmp[:, r % 2, :], h_ps[2 * (r % 2)][:, :], ACT.Silu).then_inc(silu, 1)

            def gate_hi(n, r):
                if peeled(n) and 1 <= n <= CB_PE:
                    act.wait_ge(weighed, n)
                else:
                    act.wait_ge(gated, n + 1)
                if not (peeled(n) and n < 2):
                    act.wait_ge(w2_mm, n - 1)
                act.copy(pT_flat[:, r % 2, 0:T], rtmp[:, 4 + r % 2, :]).then_inc(g_hi, 1)

            def hi_and_silu(n, r, _):
                gate_hi(n, r)
                if not (peeled(n) and n + 2 >= NX):
                    silus(n + 2, r)

            silus(0, 0)
            silus(1, 1)
            gate_hi(0, 0)
            silus(2, 2)
            act.wait_ge(ct_mm, 1)
            act.copy(combT, g_ps[0:E, :]).then_inc(ct_sb, 1)
            over_experts(act, 1, hi_and_silu)
            act.wait_ge(w2_mm, NX)
            act.copy(prob[:, 0, :], acc_ps[0][:, :]).then_inc(fin[0], 1)

        @block.vector
        def _(dve):
            links = [0]

            def link(ins):
                links[0] += 1
                ins.then_inc(chain_v, 1)
                dve.wait_ge(chain_v, links[0])

            def norm_rows(o, got, signal):
                dve.wait_ge(got, 1)
                link(dve.reciprocal(rstd[:, o:o + TT, 0], std[:, o:o + TT, 0]))
                for tt in range(TT):
                    dve.tensor_scalar(xn[:, tt, :], x_sb[:, tt, :], mv[:, o + tt, 0:1], rstd[:, o + tt, :],
                                      ALU.subtract, ALU.mult).then_inc(signal, 1)

            dve.memset(gs[:, :, :], -3.0e38)
            link(dve.memset(epsc[:, :], EPS))
            dve.wait_ge(d_x, 16)
            for tt in range(TT):
                last = dve.bn_stats(stat[:, tt, :], x_sb[:, tt, :])
            link(last)
            for tt in range(TT):
                dve.bn_aggr(mv[:, tt, :], stat[:, tt, :]).then_inc(ln_mv, 1)
            norm_rows(0, ln_std, ln_xn)

            def step(g, kind, i):
                if kind == "M":
                    u = use(g, kind, i)
                    dve.wait_ge(wk_out, u + 1)
                    for n, (hi, lo, src) in enumerate(m_parts(u, i)):
                        last = dve.tensor_tensor(lo, src, f(hi), ALU.subtract)
                    last.then_inc(m_lo, 1)
                elif kind in "BC" and NPG * g + i < ROPE_V:
                    dve.wait_ge(d_rope, 16)
                    dve.wait_ge(wk_out, use(g, kind, i) + 1)
                    rope_tile(dve, link, g, i, 0 if kind == "B" else 2, 0).then_inc(rope_a, 1)
                    dve.wait_ge(rope_a, 2 * (NPG * g + i) + "BC".index(kind) + 1)
                elif kind in "RP" and i == NQT - 1:
                    p = NPG * g + "RP".index(kind)
                    u = use(g, kind, i)
                    dve.wait_ge(wk_out, u + 1)
                    dve.tensor_tensor(qsp[R:P, p % 4, 0, :], work[u % 2][0:R, :], f(qsp[0:R, p % 4, 0, :]), ALU.subtract)
                    dve.tensor_tensor(qsp[0:R, p % 4, 1, :], work[u % 2][R:P, :], f(qsp[R:P, p % 4, 1, :]), ALU.subtract) \
                       .then_inc(q_lo, 1)

                elif kind == "X":
                    for dc in range(ND):
                        dve.wait_ge(xT_hi, dc + 1)
                        dve.tensor_tensor(xnT[:, 1, dc, :], t_ps[dc][:, :], f(xnT[:, 0, dc, :]), ALU.subtract) \
                           .then_inc(xT_lo, 1)
                elif kind == "K":
                    for n in range(2):
                        dve.wait_ge(kT_hi, n + 1)
                        dve.tensor_tensor(kdup[:, 1, n * L:(n + 1) * L], s_ps[n][:, :], f(kdup[:, 0, n * L:(n + 1) * L]),
                                          ALU.subtract).then_inc(kT_lo, 1)
                elif kind == "V":
                    dve.wait_ge(kv_roped, 1)
                    dve.tensor_copy(kvs[:, :, 0:DC], kvr[:, :, 0, :]).then_inc(kv_split, 1)
                    dve.wait_ge(kv_split, 1)
                    dve.tensor_tensor(kvs[:, :, DC:P], kvr[:, :, 0, :], f(kvs[:, :, 0:DC]), ALU.subtract) \
                       .then_inc(kv_split, 1)

            def row_max(t):
                dve.wait_ge(s_mm, t + 1)
                dve.tensor_reduce(nmax[:, t:t + 1], s_ps[t % 3][:, :], AX.X, ALU.max, negate=True).then_inc(s_max, 1)

            def inverse(t):
                dve.wait_ge(s_exp, t + 1)
                dve.reciprocal(rsum[:, t:t + 1], psum_e[:, t:t + 1]).then_inc(s_inv, 1)

            def normalise(t):
                dve.wait_ge(s_inv, t + 1)
                dve.tensor_scalar(probs[t % 4], probs[t % 4], rsum[:, t:t + 1], None, ALU.mult).then_inc(s_norm, 1)

            def prob_lo(t):
                hb, q = t // 2, slice((t % 2) * P, (t % 2 + 1) * P)
                dve.wait_ge(t_hi, t + 1)
                dve.tensor_tensor(pT[:, 1, hb % 2, :, q], t_ps[t % 2][:, :].rearrange("p (c q) -> p c q", c=LC),
                                  f(pT[:, 0, hb % 2, :, q]), ALU.subtract).then_inc(t_lo, 1)

            def ctx_sum(hb):
                h, b = divmod(hb, 2)
                dve.wait_ge(c_half, hb + 1)
                r = (h % 2) * DC
                dve.tensor_tensor(ctT[r:r + DC, h // 2, b * S:(b + 1) * S], pv_of(hb)[r:r + DC, :],
                                  ctmp[r:r + DC, hb % 2, :], ALU.add).then_inc(c_sum, 1)

            for s in PROLOGUE:
                step(*s)
            for t in range(LOOK):
                row_max(t)
            inverse(0)
            normalise(0)
            for t in range(TILES):
                if t + 1 < TILES:
                    inverse(t + 1)
                if t + LOOK < TILES:
                    row_max(t + LOOK)
                if t + 1 < TILES:
                    normalise(t + 1)
                if t >= 1:
                    prob_lo(t - 1)
                if t % 2 == 0 and t >= 4:
                    ctx_sum((t - 4) // 2)
                for s in steps(t):
                    step(*s)
            prob_lo(TILES - 1)
            ctx_sum(TILES // 2 - 2)
            ctx_sum(TILES // 2 - 1)

            def weight_hi(n, r, turns):
                dve.wait_ge(d_raw[r], 16 * turns + 16)
                if not (peeled(n) and n < SPL):
                    dve.wait_ge(w2_mm, n - SPL + 1)
                dve.tensor_copy(w_slots[r][:, 0, :], raw_v[:, r, :]).then_inc(wx_hi, 1)

            for tt in range(TT):
                if tt % 2 == 0:
                    dve.wait_ge(o_mm, tt // 2 + 1)
                dve.tensor_tensor(x_sb[:, tt, :], o_ps[tt // 2][:, (tt % 2) * D:(tt % 2 + 1) * D], x_sb[:, tt, :],
                                  ALU.add).then_inc(x1_done, 1)
                if tt >= 1:
                    dve.wait_ge(x1_done, tt)
                    dve.bn_stats(stat[:, TT + tt - 1, :], x_sb[:, tt - 1, :]).then_inc(x1_stat, 1)
            dve.wait_ge(x1_done, TT)
            dve.bn_stats(stat[:, 2 * TT - 1, :], x_sb[:, TT - 1, :]).then_inc(x1_stat, 1)
            for tt in range(TT):
                dve.wait_ge(x1_stat, tt + 1)
                dve.bn_aggr(mv[:, TT + tt, :], stat[:, TT + tt, :]).then_inc(x2_mv, 1)
            dve.wait_ge(x2_mv, TT)
            norm_rows(TT, x2_std, x2_n)
            dve.wait_ge(y_mm, TT // 2)
            dve.tensor_copy(xT_f[:, :, 2 * P:T], r_ps[1][:, :].rearrange("p (d q) -> p d q", d=ND)).then_inc(y_fv, 1)
            for k in range(TT // 2):
                dve.wait_ge(y_hi, k + 1)
                cols = slice(2 * k * P, (2 * k + 2) * P)
                dve.tensor_tensor(xnT[:, 1, :, cols], r_ps[k][:, :].rearrange("p (d q) -> p d q", d=ND),
                                  f(xnT[:, 0, :, cols]), ALU.subtract).then_inc(y_lo, 1)

            def gate(n, r):
                dve.wait_ge(h3_mm, n + 1)
                if peeled(n) and n == 0:
                    dve.wait_ge(silu, 1)
                    s = rtmp[:, 0, :]
                else:
                    dve.wait_ge(sw, n - CB_PE)
                    dve.wait_ge(g_hi, n - 1)
                    dve.wait_ge(g_lo, n - 1)
                    s = rtmp[:, 2 + r % 2, :]
                dve.tensor_tensor(rtmp[:, 4 + r % 2, :], h_ps[2 * (r % 2) + 1][:, :], s, ALU.mult).then_inc(gated, 1)

            def gate_lo(n, r):
                dve.wait_ge(g_hi, n + 1)
                dve.tensor_tensor(pT_flat[:, 2 + r % 2, 0:T], rtmp[:, 4 + r % 2, :], f(pT_flat[:, r % 2, 0:T]),
                                  ALU.subtract).then_inc(g_lo, 1)

            def gate_early(n):
                dve.wait_ge(silu, n + 1)
                dve.wait_ge(h3_mm, n + 1)
                dve.tensor_tensor(rtmp[:, 2 + n % 2, :], h_ps[2 * (n % 2) + 1][:, :], rtmp[:, n % 2, :], ALU.mult) \
                   .then_inc(gated, 1)

            def weigh(n):
                dve.wait_ge(cb_mm, n)
                dve.wait_ge(gated, n + 1)
                dve.tensor_tensor(rtmp[:, 4 + n % 2, :], cb_ps[n - 1][:, :], rtmp[:, 2 + n % 2, :], ALU.mult) \
                   .then_inc(weighed, 1)

            def route():
                dve.wait_ge(lg_sc, 1)
                link(dve.tensor_tensor(sfc[:, :, :], sc[:, :, :], bias[:, :].unsqueeze(1).to_broadcast([P, TT, E]), ALU.add))
                for tt in range(TT):
                    for g in range(G):
                        last = dve.max(g8[:, tt, g, :], sfc[:, tt, g * GE:(g + 1) * GE])
                link(last)
                link(dve.tensor_tensor(gs[:, :, 0:G], g8[:, :, :, 0], g8[:, :, :, 1], ALU.add))
                for tt in range(TT):
                    last = dve.max(gtop[:, tt, :], gs[:, tt, :])
                link(last)
                for tt in range(TT):
                    last = dve.max_index(gidx[:, tt, :], gtop[:, tt, :], gs[:, tt, :])
                link(last)
                link(dve.tensor_copy(gidxf[:, :, :], gidx[:, :, :]))
                eq = eq_v[:, 0:TT * G * TOPG].rearrange("p (t g k) -> p t g k", t=TT, k=TOPG)
                link(dve.tensor_tensor(eq, iota[:, 0:G].unsqueeze(1).unsqueeze(3).to_broadcast([P, TT, G, TOPG]),
                                       gidxf[:, :, 0:TOPG].unsqueeze(2).to_broadcast([P, TT, G, TOPG]), ALU.is_equal))
                link(dve.tensor_reduce(gmask[:, :, :], eq, AX.X, ALU.add))
                link(dve.tensor_tensor(masked[:, :, :].rearrange("p t (g e) -> p (t g) e", g=G),
                                       sfc[:, :, :].rearrange("p t (g e) -> p (t g) e", g=G),
                                       gmask[:, :, :].rearrange("p t g -> p (t g)").unsqueeze(2)
                                       .to_broadcast([P, TT * G, GE]), ALU.mult))
                link(dve.tensor_scalar(masked[:, :, :], masked[:, :, :], 0.0, None, ALU.add))
                for tt in range(TT):
                    last = dve.max(etop[:, tt, :], masked[:, tt, :])
                link(last)
                for tt in range(TT):
                    last = dve.max_index(eidx[:, tt, :], etop[:, tt, :], masked[:, tt, :])
                link(last)
                gate(0, 0)
                link(dve.tensor_copy(eidxf[:, :, :], eidx[:, :, :]))
                eq = eq_v.rearrange("p (t e k) -> p t e k", t=TT, k=TOPK)
                link(dve.tensor_tensor(eq, iota[:, :].unsqueeze(1).unsqueeze(3).to_broadcast([P, TT, E, TOPK]),
                                       eidxf[:, :, 0:TOPK].unsqueeze(2).to_broadcast([P, TT, E, TOPK]), ALU.is_equal))
                gate_lo(0, 0)
                link(dve.tensor_reduce(emask[:, :, :], eq, AX.X, ALU.add))
                link(dve.tensor_tensor(esel[:, :, :], sc[:, :, :], emask[:, :, :], ALU.mult))
                link(dve.tensor_reduce(wsum[:, :, 0], esel[:, :, :], AX.X, ALU.add))
                link(dve.tensor_scalar(wsum[:, :, 1], wsum[:, :, 0], 1e-20, None, ALU.add))
                link(dve.reciprocal(wsum[:, :, 2], wsum[:, :, 1]))
                dve.scalar_tensor_tensor(comb[:, :, :], esel[:, :, :], SCALE, wsum[:, :, 2:3].to_broadcast([P, TT, E]),
                                         ALU.mult, ALU.mult).then_inc(cmb, 1)

            dve.wait_ge(d_gate, 48)
            route()
            for n in range(1, CB_PE + 1):
                gate_early(n)

            def expert(n, r, turns):
                early = peeled(n) and n <= CB_PE
                if early:
                    if n >= 2:
                        dve.wait_ge(g_lo, n - 1)
                    weigh(n)
                if not peeled(n) or POOL_HI <= n + AHEAD < NX:
                    weight_hi(n + AHEAD, (r + AHEAD) % PERIOD, turns + (r + AHEAD) // PERIOD)
                if not early:
                    gate(n, r)
                gate_lo(n, r)

            over_experts(dve, 1, expert)
            dve.wait_ge(w2_mm, NX + 1)
            dve.tensor_copy(prob[:, 1, :], acc_ps[1][:, :]).then_inc(fin[1], 1)

        @block.gpsimd
        def _(pool):
            links = [0]

            def link(ins):
                links[0] += 1
                ins.then_inc(chain_p, 1)
                pool.wait_ge(chain_p, links[0])

            pool.wait_ge(d_kv, 32)
            hd = DC // 2
            for b in range(B):
                rows = slice(b * LC, (b + 1) * LC)
                pool.tensor_tensor(kvr[:, rows, 0, :], kv[:, rows, :], kvtab[:, :, 0, :], ALU.mult)
                pool.tensor_tensor(kvr[:, rows, 1, 0:hd], kv[:, rows, hd:DC], kvtab[:, :, 1, 0:hd], ALU.mult)
                link(pool.tensor_tensor(kvr[:, rows, 1, hd:DC], kv[:, rows, 0:hd], kvtab[:, :, 1, hd:DC], ALU.mult))
            link(pool.tensor_tensor(kvr[:, :, 0, :], kvr[:, :, 0, :], kvr[:, :, 1, :], ALU.add))
            pool.tensor_copy(kvr[:, :, 1, :], kvr[:, :, 0, :]).then_inc(kv_roped, 1)

            def ropes(g, j):
                p = NPG * g + j
                for k in range(NQT):
                    if p < ROPE_V and k != 1:
                        continue
                    pool.wait_ge(wk_out, use(g, "BBC"[k], j) + 1)
                    rope_tile(pool, link, g, j, k, 2).then_inc(rope_p, 1)
                    await_roped(pool, p, k)

            def weight_lo(n, r):
                if peeled(n) and n < POOL_HI:
                    pool.wait_ge(d_raw[n], 16)
                    if n == 0:
                        pool.wait_ge(wk_full, Q_DONE[NG - 1])
                    if n == SPL_M:
                        pool.wait_ge(s_mm, TILES)
                    link(pool.tensor_copy(w_slots[n][:, 0, :], raw_v[:, n, :]))
                else:
                    pool.wait_ge(wx_hi, n - POOL_HI + 1)
                pool.tensor_tensor(w_slots[r][:, 1, :], raw_v[:, r, :], f(w_slots[r][:, 0, :]), ALU.subtract) \
                    .then_inc(wx_lo, 1)

            def weigh(n, r, turns):
                pool.wait_ge(silu, n + 1)
                c = (r - 1) % CBR
                pool.wait_ge(d_cb[c], 16 * (turns - (r == 0) + (c >= CB_PE)))
                if peeled(n) and n - 2 <= CB_PE:
                    pool.wait_ge(weighed, n - 2)
                else:
                    pool.wait_ge(gated, n - 1)
                pool.tensor_tensor(rtmp[:, 2 + r % 2, :], rtmp[:, r % 2, :], roped_flat[:, c, :], ALU.mult) \
                    .then_inc(sw, 1)

            pool.wait_ge(d_rope, 16)
            for g in range(NG):
                for j in range(NPG):
                    ropes(g, j)
            for n in range(POOL_HI):
                weight_lo(n, n)

            def expert(n, r, turns):
                if not peeled(n) or n > CB_PE:
                    weigh(n, r, turns)
                if not peeled(n) or n + AHEAD < NX:
                    weight_lo(n + AHEAD, (r + AHEAD) % PERIOD)

            over_experts(pool, POOL_HI - AHEAD, expert)


def rope_tables(length, dim):
    inv = (np.float32(1.0) / np.float32(10000.0) ** (np.arange(0, dim, 2, dtype=np.float32) / np.float32(dim)))
    f = np.arange(length, dtype=np.float32)[:, None] * inv.astype(np.float32)[None, :]
    return np.repeat(np.sin(f), 2, axis=-1), np.repeat(np.cos(f), 2, axis=-1)


def tile_rows():
    n = P - HALF
    ab = [[(0, h * HALF + i) for i in range(HALF)] + [(1, h * HALF + i) for i in range(n)] for h in range(2)]
    c = [(1, h * HALF + i) for h in range(2) for i in range(n, HALF)]
    return [np.array(t) for t in (ab[0], ab[1], c)]


def kernel(x, ctx_512, L0_xattn_Wq, L0_xattn_w_kc_q, L0_xattn_w_kc_kv, L0_xattn_W_qr, L0_xattn_W_kr, L0_xattn_Wo,
           L0_ffn_gate_weight, L0_ffn_e_score_correction_bias, L0_ffn_w1, L0_ffn_w3, L0_ffn_w2, L0_ffn_ws1,
           L0_ffn_ws3, L0_ffn_ws2):
    import concourse.bacc as bacc
    from concourse.bass_utils import run_bass_kernel_spmd

    a = np.asarray
    c = np.ascontiguousarray
    f32 = np.float32
    x_l = c(a(x).reshape(TT, P, D).transpose(1, 0, 2))
    kv_l = c(a(ctx_512).reshape(B * LC, P, DC).transpose(1, 0, 2))
    w_attn = np.zeros((NG, P, WGRP), f32)
    wq = a(L0_xattn_Wq).reshape(NG, HG, K, D)
    wkcq = a(L0_xattn_w_kc_q).reshape(NG, HG, K, CQ)
    w_attn[:, :, 0:WM] = np.concatenate([wq, wkcq], axis=3).transpose(0, 2, 1, 3).reshape(NG, K, WM)
    wqr, wkr = a(L0_xattn_W_qr), a(L0_xattn_W_kr)
    rows = tile_rows()
    for g in range(NG):
        for j in range(NPG):
            for k in range(NQT):
                for i in range(2):
                    own = np.nonzero(rows[k][:, 0] == i)[0]
                    w_attn[g, i * R:(i + 1) * R, WM + (j * NQT + k) * P + own] = \
                        wqr[g * HG + 2 * j + i, rows[k][own, 1], :]
        for j in range(NPG):
            for i in range(2):
                col = WM + NPG * NQT * P + j * P + i * DC
                w_attn[g, i * R:(i + 1) * R, col:col + DC] = wkr[g * HG + 2 * j + i].T
    o = WM + WG
    w_attn[:, :, o:o + HG * DC] = a(L0_xattn_w_kc_kv).reshape(NG, HG, K, DC).transpose(0, 2, 1, 3).reshape(NG, K, HG * DC)
    w_attn[:, :, o + HG * DC:] = a(L0_xattn_Wo).T.reshape(NG, HG, K, D).transpose(0, 2, 1, 3).reshape(NG, K, HG * D)
    gate_l = c(a(L0_ffn_gate_weight).T.reshape(ND, P, E).transpose(1, 0, 2))
    bias_l = c(np.broadcast_to(a(L0_ffn_e_score_correction_bias), (P, E)))
    w1 = np.concatenate([a(L0_ffn_ws1)[None], a(L0_ffn_w1)])
    w3 = np.concatenate([a(L0_ffn_ws3)[None], a(L0_ffn_w3)])
    w2 = np.concatenate([a(L0_ffn_ws2)[None], a(L0_ffn_w2)])
    w_exp = np.concatenate([w.transpose(0, 2, 1).reshape(NX, ND, P, I).transpose(0, 2, 1, 3).reshape(NX, P, ND * I)
                            for w in (w1, w3)] + [w2.transpose(0, 2, 1)], axis=2)

    sin_q, cos_q = rope_tables(S, CQ)
    rope_q = np.zeros((P, NQT, 2, S), f32)
    for k in range(NQT):
        col = rows[k][:, 1]
        rope_q[:, k, 0] = cos_q.T[col]
        rope_q[:, k, 1] = sin_q.T[col] * np.where(col < HALF, f32(-1), f32(1))[:, None]
    sin_k, cos_k = rope_tables(L, DC)
    sign = np.where(np.arange(DC) < DC // 2, f32(-1), f32(1))
    rope_kv = c(np.stack([cos_k, sin_k * sign], 1).reshape(LC, P, 2, DC).transpose(1, 0, 2, 3).astype(f32))
    ident = np.eye(P, dtype=f32)
    iota = c(np.broadcast_to(np.arange(E, dtype=f32), (P, E)))

    nc = bacc.Bacc("TRN2", target_bir_lowering=False, num_devices=1)
    arrays = {"x": x_l, "ctx_kv": kv_l, "w_attn": w_attn, "w_gate": gate_l, "gate_bias": bias_l, "w_exp": c(w_exp),
              "rope_q": rope_q, "rope_kv": rope_kv, "ident": ident, "iota": iota}
    aps = [nc.dram_tensor(f"in_{n}", v.shape, mybir.dt.from_np(v.dtype), kind="ExternalInput").ap()
           for n, v in arrays.items()]
    c_dram = nc.dram_tensor("combine_scratch", (E, T), F32, kind="Internal").ap()
    out = nc.dram_tensor("out_T", (D, T), F32, kind="ExternalOutput").ap()
    build(nc, *aps, c_dram, out)
    r = run_bass_kernel_spmd(nc, [{f"in_{n}": v for n, v in arrays.items()}], core_ids=[0])
    return r.results[0]["out_T"].T.reshape(B, S, D)
```
